# Optimizing a Trainium2 kernel written in Bass

```python
import numpy as np
import jax
import jax.numpy as jnp

def _softmax(x, axis=-1):
    return jax.nn.softmax(x, axis=axis)

def _gelu(x):
    return jax.nn.gelu(x, approximate=True)

def _silu(x):
    return jax.nn.silu(x)

def _sigmoid(x):
    return jax.nn.sigmoid(x)

def _layernorm(x, axis=-1, eps=1e-05):
    m = jnp.mean(x, axis=axis, keepdims=True)
    v = jnp.var(x, axis=axis, keepdims=True)
    return (x - m) / jnp.sqrt(v + eps)

def _scatter_add(tgt, idx, src, axis=0):
    return tgt.at[idx].add(src)

def _segment_sum(src, seg, n):
    return jax.ops.segment_sum(src, seg, n)
kernel_name = 'mk_seq_preln_d1_jaxref_r4_a13de0'

def setup_inputs(seed: int=0):
    np.random.seed(seed)
    _w = jnp.asarray

    def _L0_attn_setup():
        import jax, jax.numpy as jnp
        import numpy as np
        import math
        B, N, D = (64, 128, 256)
        SHELL_DIM, RFF_DIM, ORDER = (64, 32, 4)
        CHARGE_COUPLING, SHELL_COUPLING = (1.0, 0.5)
        DIST_COUPLING, DIST_SCALE = (0.3, 10.0)
        COMBINED_DIM = 64

        def _forward(x, W_charge, b_charge, W_shell, b_shell, omega, rff_bias, W_combine, W_v, b_v, W_out, b_out, log_temp):
            b, n, d = x.shape
            q = jnp.tanh(x @ W_charge.T + b_charge)[..., 0]
            coeffs = jnp.asarray([(-CHARGE_COUPLING) ** m / math.factorial(m) for m in range(ORDER + 1)], dtype=x.dtype)
            mags = jnp.sqrt(jnp.abs(coeffs) + 1e-10)
            phi_c = mags * q[..., None] ** jnp.arange(ORDER + 1)
            shell = x @ W_shell.T + b_shell
            shell = shell / jnp.maximum(jnp.linalg.norm(shell, axis=-1, keepdims=True), 1e-12)
            proj = shell @ omega.T + rff_bias
            rff_scale = math.sqrt(2.0 / (2 * RFF_DIM)) * math.sqrt(math.exp(-SHELL_COUPLING))
            phi_s = jnp.concatenate([jnp.cos(proj), jnp.sin(proj)], axis=-1) * rff_scale
            tp = (phi_c[..., :, None] * phi_s[..., None, :]).reshape(b, n, -1)
            phi = tp @ W_combine.T
            idx = jnp.arange(n)
            T = jnp.exp(-DIST_COUPLING * jnp.abs(idx[:, None] - idx[None, :]).astype(x.dtype) / DIST_SCALE)
            temp = jax.nn.softplus(log_temp) + 0.1
            logits = jnp.einsum('bnd,bmd->bnm', phi, phi) * T / temp
            causal = idx[:, None] >= idx[None, :]
            logits = jnp.where(causal, logits, -jnp.inf)
            attn = jax.nn.softmax(logits, axis=-1)
            V = x @ W_v.T + b_v
            out = jnp.einsum('bnm,bmd->bnd', attn, V)
            return out @ W_out.T + b_out
        key = jax.random.key(seed)
        ks = jax.random.split(key, 12)
        s = 0.02
        inp = {'x': jax.random.normal(ks[0], (B, N, D), dtype=jnp.float32), 'W_charge': jax.random.normal(ks[1], (1, D), dtype=jnp.float32) * s, 'b_charge': jnp.zeros((1,), dtype=jnp.float32), 'W_shell': jax.random.normal(ks[2], (SHELL_DIM, D), dtype=jnp.float32) * s, 'b_shell': jnp.zeros((SHELL_DIM,), dtype=jnp.float32), 'omega': jax.random.normal(ks[3], (RFF_DIM, SHELL_DIM), dtype=jnp.float32) * math.sqrt(SHELL_COUPLING), 'rff_bias': jax.random.uniform(ks[4], (RFF_DIM,), dtype=jnp.float32) * (2.0 * math.pi), 'W_combine': jax.random.normal(ks[5], (COMBINED_DIM, (ORDER + 1) * 2 * RFF_DIM), dtype=jnp.float32) * s, 'W_v': jax.random.normal(ks[6], (D, D), dtype=jnp.float32) * s, 'b_v': jnp.zeros((D,), dtype=jnp.float32), 'W_out': jax.random.normal(ks[7], (D, D), dtype=jnp.float32) * s, 'b_out': jnp.zeros((D,), dtype=jnp.float32), 'log_temp': jnp.zeros((), dtype=jnp.float32)}
        return inp
    _L0_attn_in = _L0_attn_setup()

    def _L0_ffn_setup():
        import jax, jax.numpy as jnp
        import numpy as np
        D_MODEL = 256
        NUM_SLOTS = 64
        TOP_K = 8
        B, T = (4, 1024)

        def _forward(x, slot_init, slot_scale, w1, b1, w2, b2, gru_wih, gru_whh, gru_bih, gru_bhh, wv, bv, wo, bo, tau):
            Bn, Tn, D = x.shape
            Sn = slot_init.shape[0]
            S = jnp.broadcast_to((slot_init * slot_scale)[None], (Bn, Sn, D)).astype(x.dtype)
            slot_mean = S.mean(axis=1, keepdims=True)
            ctx = jnp.concatenate([x, jnp.broadcast_to(slot_mean, x.shape)], axis=-1)
            h = jax.nn.gelu(ctx @ w1.T + b1, approximate=False)
            route_logits = (h @ w2.T + b2) / (jnp.abs(tau) + 0.1)
            topk_vals, topk_idx = jax.lax.top_k(route_logits, TOP_K)
            topk_w = jax.nn.softmax(topk_vals, axis=-1)
            alpha = jnp.sum(topk_w[..., None] * jax.nn.one_hot(topk_idx, Sn, dtype=x.dtype), axis=-2)
            slot_input = jnp.einsum('bts,btd->bsd', alpha, x)
            slot_wsum = alpha.sum(axis=1) + 1e-08
            gi = (slot_input / slot_wsum[..., None]).reshape(Bn * Sn, D)
            hs = S.reshape(Bn * Sn, D)
            gx = gi @ gru_wih.T + gru_bih
            gh = hs @ gru_whh.T + gru_bhh
            xr, xz, xn = jnp.split(gx, 3, axis=-1)
            hr, hz, hn = jnp.split(gh, 3, axis=-1)
            r = jax.nn.sigmoid(xr + hr)
            z = jax.nn.sigmoid(xz + hz)
            n = jnp.tanh(xn + r * hn)
            h_new = (1.0 - z) * n + z * hs
            S_new = h_new.reshape(Bn, Sn, D)
            slot_values = S_new @ wv.T + bv
            out = jnp.einsum('bts,bsd->btd', alpha, slot_values)
            return out @ wo.T + bo
        key = jax.random.key(seed)
        ks = jax.random.split(key, 16)
        D, S = (D_MODEL, NUM_SLOTS)
        H = D // 2
        sc = lambda fan_in: 1.0 / np.sqrt(fan_in)
        inp = {'x': jax.random.normal(ks[0], (B, T, D), dtype=jnp.float32), 'slot_init': jax.random.normal(ks[1], (S, D), dtype=jnp.float32) * 0.1, 'slot_scale': jnp.ones((S, 1), dtype=jnp.float32), 'w1': jax.random.normal(ks[2], (H, 2 * D), dtype=jnp.float32) * sc(2 * D), 'b1': jnp.zeros((H,), dtype=jnp.float32), 'w2': jax.random.normal(ks[3], (S, H), dtype=jnp.float32) * sc(H), 'b2': jnp.zeros((S,), dtype=jnp.float32), 'gru_wih': jax.random.normal(ks[4], (3 * D, D), dtype=jnp.float32) * sc(D), 'gru_whh': jax.random.normal(ks[5], (3 * D, D), dtype=jnp.float32) * sc(D), 'gru_bih': jnp.zeros((3 * D,), dtype=jnp.float32), 'gru_bhh': jnp.zeros((3 * D,), dtype=jnp.float32), 'wv': jax.random.normal(ks[6], (D, D), dtype=jnp.float32) * sc(D), 'bv': jnp.zeros((D,), dtype=jnp.float32), 'wo': jax.random.normal(ks[7], (D, D), dtype=jnp.float32) * sc(D), 'bo': jnp.zeros((D,), dtype=jnp.float32), 'tau': jnp.ones((1,), dtype=jnp.float32)}
        return inp
    _L0_ffn_in = _L0_ffn_setup()
    _d = {'L0_attn_x': _L0_attn_in['x'], 'L0_attn_W_charge': _L0_attn_in['W_charge'], 'L0_attn_b_charge': _L0_attn_in['b_charge'], 'L0_attn_W_shell': _L0_attn_in['W_shell'], 'L0_attn_b_shell': _L0_attn_in['b_shell'], 'L0_attn_omega': _L0_attn_in['omega'], 'L0_attn_rff_bias': _L0_attn_in['rff_bias'], 'L0_attn_W_combine': _L0_attn_in['W_combine'], 'L0_attn_W_v': _L0_attn_in['W_v'], 'L0_attn_b_v': _L0_attn_in['b_v'], 'L0_attn_W_out': _L0_attn_in['W_out'], 'L0_attn_b_out': _L0_attn_in['b_out'], 'L0_attn_log_temp': _L0_attn_in['log_temp'], 'L0_ffn_slot_init': _L0_ffn_in['slot_init'], 'L0_ffn_slot_scale': _L0_ffn_in['slot_scale'], 'L0_ffn_w1': _L0_ffn_in['w1'], 'L0_ffn_b1': _L0_ffn_in['b1'], 'L0_ffn_w2': _L0_ffn_in['w2'], 'L0_ffn_b2': _L0_ffn_in['b2'], 'L0_ffn_gru_wih': _L0_ffn_in['gru_wih'], 'L0_ffn_gru_whh': _L0_ffn_in['gru_whh'], 'L0_ffn_gru_bih': _L0_ffn_in['gru_bih'], 'L0_ffn_gru_bhh': _L0_ffn_in['gru_bhh'], 'L0_ffn_wv': _L0_ffn_in['wv'], 'L0_ffn_bv': _L0_ffn_in['bv'], 'L0_ffn_wo': _L0_ffn_in['wo'], 'L0_ffn_bo': _L0_ffn_in['bo'], 'L0_ffn_tau': _L0_ffn_in['tau']}
    _x0 = _d['L0_attn_x']
    _d['L0_attn_x'] = jax.random.normal(jax.random.fold_in(jax.random.key(seed), 1), (32, 512, 256), dtype=_x0.dtype)
    del _x0
    return _d

def reference(L0_attn_x, L0_attn_W_charge, L0_attn_b_charge, L0_attn_W_shell, L0_attn_b_shell, L0_attn_omega, L0_attn_rff_bias, L0_attn_W_combine, L0_attn_W_v, L0_attn_b_v, L0_attn_W_out, L0_attn_b_out, L0_attn_log_temp, L0_ffn_slot_init, L0_ffn_slot_scale, L0_ffn_w1, L0_ffn_b1, L0_ffn_w2, L0_ffn_b2, L0_ffn_gru_wih, L0_ffn_gru_whh, L0_ffn_gru_bih, L0_ffn_gru_bhh, L0_ffn_wv, L0_ffn_bv, L0_ffn_wo, L0_ffn_bo, L0_ffn_tau):

    def _L0_attn_ref(x, W_charge, b_charge, W_shell, b_shell, omega, rff_bias, W_combine, W_v, b_v, W_out, b_out, log_temp):
        import jax, jax.numpy as jnp
        import numpy as np
        import math
        B, N, D = (64, 128, 256)
        SHELL_DIM, RFF_DIM, ORDER = (64, 32, 4)
        CHARGE_COUPLING, SHELL_COUPLING = (1.0, 0.5)
        DIST_COUPLING, DIST_SCALE = (0.3, 10.0)
        COMBINED_DIM = 64

        def _forward(x, W_charge, b_charge, W_shell, b_shell, omega, rff_bias, W_combine, W_v, b_v, W_out, b_out, log_temp):
            b, n, d = x.shape
            q = jnp.tanh(x @ W_charge.T + b_charge)[..., 0]
            coeffs = jnp.asarray([(-CHARGE_COUPLING) ** m / math.factorial(m) for m in range(ORDER + 1)], dtype=x.dtype)
            mags = jnp.sqrt(jnp.abs(coeffs) + 1e-10)
            phi_c = mags * q[..., None] ** jnp.arange(ORDER + 1)
            shell = x @ W_shell.T + b_shell
            shell = shell / jnp.maximum(jnp.linalg.norm(shell, axis=-1, keepdims=True), 1e-12)
            proj = shell @ omega.T + rff_bias
            rff_scale = math.sqrt(2.0 / (2 * RFF_DIM)) * math.sqrt(math.exp(-SHELL_COUPLING))
            phi_s = jnp.concatenate([jnp.cos(proj), jnp.sin(proj)], axis=-1) * rff_scale
            tp = (phi_c[..., :, None] * phi_s[..., None, :]).reshape(b, n, -1)
            phi = tp @ W_combine.T
            idx = jnp.arange(n)
            T = jnp.exp(-DIST_COUPLING * jnp.abs(idx[:, None] - idx[None, :]).astype(x.dtype) / DIST_SCALE)
            temp = jax.nn.softplus(log_temp) + 0.1
            logits = jnp.einsum('bnd,bmd->bnm', phi, phi) * T / temp
            causal = idx[:, None] >= idx[None, :]
            logits = jnp.where(causal, logits, -jnp.inf)
            attn = jax.nn.softmax(logits, axis=-1)
            V = x @ W_v.T + b_v
            out = jnp.einsum('bnm,bmd->bnd', attn, V)
            return out @ W_out.T + b_out
        return _forward(x, W_charge, b_charge, W_shell, b_shell, omega, rff_bias, W_combine, W_v, b_v, W_out, b_out, log_temp)

    def _L0_ffn_ref(x, slot_init, slot_scale, w1, b1, w2, b2, gru_wih, gru_whh, gru_bih, gru_bhh, wv, bv, wo, bo, tau):
        import jax, jax.numpy as jnp
        import numpy as np
        D_MODEL = 256
        NUM_SLOTS = 64
        TOP_K = 8
        B, T = (4, 1024)

        def _forward(x, slot_init, slot_scale, w1, b1, w2, b2, gru_wih, gru_whh, gru_bih, gru_bhh, wv, bv, wo, bo, tau):
            Bn, Tn, D = x.shape
            Sn = slot_init.shape[0]
            S = jnp.broadcast_to((slot_init * slot_scale)[None], (Bn, Sn, D)).astype(x.dtype)
            slot_mean = S.mean(axis=1, keepdims=True)
            ctx = jnp.concatenate([x, jnp.broadcast_to(slot_mean, x.shape)], axis=-1)
            h = jax.nn.gelu(ctx @ w1.T + b1, approximate=False)
            route_logits = (h @ w2.T + b2) / (jnp.abs(tau) + 0.1)
            topk_vals, topk_idx = jax.lax.top_k(route_logits, TOP_K)
            topk_w = jax.nn.softmax(topk_vals, axis=-1)
            alpha = jnp.sum(topk_w[..., None] * jax.nn.one_hot(topk_idx, Sn, dtype=x.dtype), axis=-2)
            slot_input = jnp.einsum('bts,btd->bsd', alpha, x)
            slot_wsum = alpha.sum(axis=1) + 1e-08
            gi = (slot_input / slot_wsum[..., None]).reshape(Bn * Sn, D)
            hs = S.reshape(Bn * Sn, D)
            gx = gi @ gru_wih.T + gru_bih
            gh = hs @ gru_whh.T + gru_bhh
            xr, xz, xn = jnp.split(gx, 3, axis=-1)
            hr, hz, hn = jnp.split(gh, 3, axis=-1)
            r = jax.nn.sigmoid(xr + hr)
            z = jax.nn.sigmoid(xz + hz)
            n = jnp.tanh(xn + r * hn)
            h_new = (1.0 - z) * n + z * hs
            S_new = h_new.reshape(Bn, Sn, D)
            slot_values = S_new @ wv.T + bv
            out = jnp.einsum('bts,bsd->btd', alpha, slot_values)
            return out @ wo.T + bo
        return _forward(x, slot_init, slot_scale, w1, b1, w2, b2, gru_wih, gru_whh, gru_bih, gru_bhh, wv, bv, wo, bo, tau)
    x = L0_attn_x
    x = x + _L0_attn_ref(_layernorm(x, axis=-1), L0_attn_W_charge, L0_attn_b_charge, L0_attn_W_shell, L0_attn_b_shell, L0_attn_omega, L0_attn_rff_bias, L0_attn_W_combine, L0_attn_W_v, L0_attn_b_v, L0_attn_W_out, L0_attn_b_out, L0_attn_log_temp)
    x = x + _L0_ffn_ref(_layernorm(x, axis=-1), L0_ffn_slot_init, L0_ffn_slot_scale, L0_ffn_w1, L0_ffn_b1, L0_ffn_w2, L0_ffn_b2, L0_ffn_gru_wih, L0_ffn_gru_whh, L0_ffn_gru_bih, L0_ffn_gru_bhh, L0_ffn_wv, L0_ffn_bv, L0_ffn_wo, L0_ffn_bo, L0_ffn_tau)
    return x

_drawn_inputs = setup_inputs


def setup_inputs(seed=0):
    import zlib

    import numpy as np

    out = dict(_drawn_inputs(seed))
    spreads = {'L0_attn_b_shell': (0.0, 0.8),
     'L0_attn_b_v': (0.0, 0.1),
     'L0_attn_b_out': (0.0, 0.1),
     'L0_ffn_slot_scale': (1.0, 0.6),
     'L0_ffn_b1': (0.0, 0.519),
     'L0_ffn_b2': (0.0, 0.441),
     'L0_ffn_gru_bih': (0.0, 0.1),
     'L0_ffn_gru_bhh': (0.0, 0.369),
     'L0_ffn_bv': (0.0, 0.1),
     'L0_ffn_bo': (0.0, 0.1)}
    factors = {'L0_attn_W_charge': 8.0,
     'L0_attn_W_shell': 8.0,
     'L0_attn_omega': 8.0,
     'L0_attn_rff_bias': 8.0,
     'L0_attn_W_combine': 8.0,
     'L0_attn_W_v': 4.549,
     'L0_ffn_gru_whh': 6.064}
    for name, (base, spread) in spreads.items():
        noise = np.random.default_rng([zlib.crc32(name.encode()), seed]).standard_normal(out[name].shape)
        drawn = base * np.exp(spread * noise) if base else spread * noise
        out[name] = jnp.asarray(drawn.astype(out[name].dtype))
    for name, factor in factors.items():
        out[name] = (out[name] * factor).astype(out[name].dtype)
    return out
```

```python
import numpy as np
import concourse.bass as bass
from concourse import mybir
from contextlib import ExitStack

B, N, D = 32, 512, 256
S, H, R, C = 64, 128, 32, 64
ORDER = 4
FP = mybir.dt.float32
BF = mybir.dt.bfloat16
ALU = mybir.AluOpType
ACT = mybir.ActivationFunctionType
AX = mybir.AxisListType
MAGIC = 12582912.0
TWO_PI = 6.283185307179586
PI_HI = 6.28125
PI_LO = TWO_PI - PI_HI
PI_CLAMP = 3.1415925
FEATS = 353


class Queues:

    def __init__(self, nc, ctx):
        self.nc, self.ctx = nc, ctx
        self.lists = {k: [] for k in ("pe", "act", "dve", "pool", "sp")}
        self.sems, self.counts, self.at, self.seen = {}, {}, {}, {}

    def sem(self, name):
        if name not in self.sems:
            self.sems[name] = self.ctx.enter_context(self.nc.semaphore("s_" + name))
            self.counts[name] = 0
        return self.sems[name]

    def need(self, eng, *products):
        for name, n in products:
            if n < 0:
                continue
            sem, value = self.at[(name, n)]
            if self.seen.get((eng, sem), 0) >= value:
                continue
            self.seen[(eng, sem)] = value
            s = self.sems[sem]
            self.lists[eng].append(lambda e, s=s, v=value: e.wait_ge(s, v))

    def put(self, eng, fn, name=None, n=0, sem=None, by=1):
        if name is None:
            self.lists[eng].append(fn)
            return
        sem = sem or name
        s = self.sem(sem)
        self.counts[sem] += by
        self.at[(name, n)] = (sem, self.counts[sem])
        self.lists[eng].append(lambda e: fn(e).then_inc(s, by))


class Banks:

    def __init__(self, q, tensors):
        self.q, self.tensors, self.n = q, tensors, 0
        self.freed = [None] * len(tensors)

    def take(self):
        i = self.n % len(self.tensors)
        self.n += 1
        if self.freed[i] is not None:
            self.q.need("pe", self.freed[i])
        self.freed[i] = None
        return i, self.tensors[i]


def build(nc, a, out):
    ctx = ExitStack()
    with ctx:
        q = Queues(nc, ctx)
        need, put = q.need, q.put

        def sb(name, shape, dt=FP):
            return ctx.enter_context(nc.sbuf_tensor(name, shape, dt))

        banks = [ctx.enter_context(nc.psum_tensor(f"ps{i}", [128, 512], FP)) for i in range(8)]
        T = Banks(q, banks[0:2])
        L = Banks(q, banks[2:4])
        G = Banks(q, banks[4:6])
        O = Banks(q, banks[6:8])

        ident = sb("ident", [128, 128])
        identb = sb("identb", [128, 128], BF)
        maskb = sb("maskb", [128, 128], BF)
        ones = sb("ones", [128, 128])
        W1 = sb("W1", [128, 2, FEATS])
        biasM = sb("biasM", [128, FEATS])
        biasC = sb("biasC", [128, 2, R])
        wc = sb("wc", [128, 3, C])
        wcs = sb("wcs", [128, 3])
        U = sb("U", [C, N])
        Wk = sb("Wk", [C, N])
        w1a = sb("w1a", [128, 2, H])
        b1 = sb("b1", [128, 1])
        w2 = sb("w2", [128, S])
        b2 = sb("b2", [128, S])
        wih = sb("wih", [128, 2, 3 * D])
        GH = sb("GH", [128, 6, S])
        HN = sb("HN", [128, 2, S])
        bihn = sb("bihn", [128, 6])
        S0 = sb("S0", [128, 2, S])
        Wvo = sb("Wvo", [128, 2, D])
        bSV = sb("bSV", [128, D])
        half = sb("half", [128, 8])
        scr = sb("scr", [128, 64])

        NX = 6
        X = sb("X", [128, NX, 4, D])
        stats = sb("stats", [128, 2, 4, 6])
        mv = sb("mv", [128, 2, 4, 2])
        rs = sb("rs", [128, 2, 3, 4])
        xn = sb("xn", [128, 2, 4, D])
        xnT = sb("xnT", [128, 2, 2, N])
        VS = sb("VS", [128, 4, 4, FEATS])
        tg = sb("tg", [128, 2, 4, 2 * R])
        tg2 = sb("tg2", [128, 2, 4, 2 * R])
        qq = sb("qq", [128, 2, 4, 4])
        n2 = sb("n2", [128, 2, 2, 4])
        tp = sb("tp", [128, 1, 4, 5, 64])
        tpT = sb("tpT", [128, 1, 3, N])
        QT = sb("QT", [C, 4, N])
        KT = sb("KT", [C, 4, N])
        nmax = sb("nmax", [128, 8])
        rsum = sb("rsum", [128, 8])
        rinv = sb("rinv", [128, 8])
        E = sb("E", [128, 2, N])
        ET = sb("ET", [128, 2, N])
        NY = 6
        x1 = sb("x1", [128, NY, 4, D])
        stats2 = sb("stats2", [128, 2, 4, 6])
        mv2 = sb("mv2", [128, 2, 4, 2])
        rs2 = sb("rs2", [128, 2, 3, 4])
        xm = sb("xm", [128, 2, 4, D])
        xmT = sb("xmT", [128, 1, 2, N])
        hT = sb("hT", [128, 2, N])
        lg = sb("lg", [128, 2, 2, 4, S])
        m8 = sb("m8", [128, 2, 4, 8])
        ex = sb("ex", [128, 2, 2, 4, S])
        asum = sb("asum", [128, 2, 2, 4])
        AL = sb("AL", [128, 2, 4, 2, S])
        alt = sb("alt", [128, 2, S])
        rw = sb("rw", [128, S])
        GI = sb("GI", [128, 2, 2, 2, S])
        grz = sb("grz", [128, 4, 2, S])
        gn = sb("gn", [128, 2, 2, S])
        gt = sb("gt", [128, 2, 2, S])
        SN = sb("SN", [128, 2, 2, S])
        SV = sb("SV", [128, 2, D])
        aT = sb("aT", [128, 2, N])

        wv_n = x1[:, 0, 0:2, :]
        woT = x1[:, 0, 2:4, :]
        fwv = x1[:, 1, 0:2, :]
        fwoT = x1[:, 1, 2:4, :]
        whh = x1[:, 2:4, :, :].rearrange("p a t d -> p (a t d)")[:, 0:2 * 3 * D].rearrange("p (c n) -> p c n", c=2)
        stg = x1[:, 4, :, :].rearrange("p t d -> p (t d)")
        bvc = stg[:, 0:2]
        boutr = stg[0:1, 8:8 + D]
        fbvc = stg[:, 2:4]
        fbor = stg[0:1, 264:264 + D]
        wsh = stg[0:64, 520:776]
        omT = stg[0:64, 776:808]
        bshc = stg[0:64, 808:809]
        brow = stg[0:1, 812:812 + 65]
        rbB = stg[:, 880:912]
        mslot = stg[:, 912:914]
        bhh = stg[:, 914:920]
        ltb = stg[:, 920:921]
        taub = stg[:, 921:922]
        tmp8 = stg[:, 922:938]
        stg2 = x1[:, 5, :, :].rearrange("p t d -> p (t d)")
        w1b = stg2[:, 0:2 * H].rearrange("p (c n) -> p c n", c=2)
        sscale = stg2[:, 256:320]
        bcA = stg2[:, 320:320 + 256].rearrange("p (c n) -> p c n", c=2)
        bcB = stg2[:, 576:576 + 256].rearrange("p (c n) -> p c n", c=2)
        bcS = stg2[0:64, 832:960]
        b2raw = stg2[:, 960:1024]

        def load(dst, src):
            put("sp", lambda e, d=dst, s=src: e.dma_start(d, s), "w", 0, by=16)

        def chunks(ap, c=2):
            return ap.rearrange("(c p) n -> p c n", c=c)

        def load_x(b):
            need("sp", ("x1", b - NX))
            put("sp", lambda e, b=b: e.dma_start(X[:, b % NX, :, :], a["x"][b].rearrange("(t p) d -> p t d", p=128)),
                "x", b, sem=f"x{b % NX}", by=16)

        load_x(0)
        load(wv_n, chunks(a["W_v"]))
        load(woT, chunks(a["W_outT"]))
        load(wsh, a["W_shell"])
        load(omT, a["omegaT"])
        load(bshc, a["b_shell"].rearrange("(p a) -> p a", a=1))
        load(brow[:, 0:64], a["b_shell"].rearrange("(a n) -> a n", a=1))
        load(brow[:, 64:65], a["b_charge"].rearrange("(a n) -> a n", a=1))
        load(W1[:, :, 256:321], chunks(a["W_scT"]))
        load(bvc, a["b_v"])
        load(boutr, a["b_out"].rearrange("(a n) -> a n", a=1))
        load(rbB, a["rff_bias"].partition_broadcast(128))
        load(wc[:, 0:2, :], a["W_combineT"][0:256, :].rearrange("(c p) n -> p c n", c=2))
        load(wc[0:64, 2, :], a["W_combineT"][256:320, :])
        load(U[:, :], a["decay"][0, :].partition_broadcast(C))
        load(Wk[:, :], a["decay"][1, :].partition_broadcast(C))
        load(ltb, a["log_temp"].partition_broadcast(128))
        load_x(1)
        load(fwv, chunks(a["wv"]))
        load(fwoT, chunks(a["woT"]))
        load(fbvc, a["bv"])
        load(fbor, a["bo"].rearrange("(a n) -> a n", a=1))
        load(whh, chunks(a["gru_whhT"]))
        load(wih[:, :, :], chunks(a["gru_wihT"]))
        load(w1a[:, :, :], chunks(a["w1T"][0:256, :]))
        load(w1b, chunks(a["w1T"][256:512, :]))
        load(b1[:, :], a["b1"].rearrange("(p a) -> p a", a=1))
        load(w2[:, :], a["w2T"])
        load(b2raw, a["b2"].partition_broadcast(128))
        load(bihn[:, :], a["gru_bih"])
        load(bhh, a["gru_bhh"])
        load(S0[:, :, :], chunks(a["slot_initT"]))
        load(sscale, a["slot_scale"].partition_broadcast(128))
        load(taub, a["tau"].partition_broadcast(128))
        for b in range(2, 4):
            load_x(b)

        chain = [0]

        def pool(fn, last=None):
            if chain[0]:
                need("pool", ("cp", chain[0] - 1))
            put("pool", fn, "cp", chain[0])
            chain[0] += 1

        pool(lambda e: e.memset(ident[:, :], 0.0))
        pool(lambda e: e.affine_select(out=ident[:, :], in_=ident[:, :], compare_op=ALU.not_equal, fill=1.0,
                                       base=0, pattern=[[-1, 128]], channel_multiplier=1))
        pool(lambda e: e.memset(identb[:, :], 0.0))
        pool(lambda e: e.affine_select(out=identb[:, :], in_=identb[:, :], compare_op=ALU.not_equal, fill=1.0,
                                       base=0, pattern=[[-1, 128]], channel_multiplier=1))
        pool(lambda e: e.memset(maskb[:, :], 0.0))
        pool(lambda e: e.affine_select(out=maskb[:, :], in_=maskb[:, :], compare_op=ALU.is_ge, fill=-1e30,
                                       base=0, pattern=[[-1, 128]], channel_multiplier=1))
        pool(lambda e: e.memset(ones[:, :], 1.0))
        pool(lambda e: e.memset(half[:, :], -0.5))
        mags = [float(np.sqrt(np.float32(1.0 / f) + np.float32(1e-10))) for f in (1, 1, 2, 6, 24)]
        rff = float(np.sqrt(2.0 / (2 * R)) * np.sqrt(np.exp(-0.5)))
        for m in range(5):
            pool(lambda e, m=m: e.memset(wcs[64 * (m % 2):64 * (m % 2) + 64, m // 2:m // 2 + 1], mags[m] * rff))
        need("pool", ("w", 0))
        t8 = lambda i: tmp8[:, i:i + 1]
        pool(lambda e: e.tensor_scalar(t8(0), ltb, -1.0, None, ALU.mult))
        pool(lambda e: e.tensor_tensor(t8(1), ltb, t8(0), ALU.subtract))
        pool(lambda e: e.tensor_scalar(t8(0), ltb, 0.0, None, ALU.max))
        pool(lambda e: e.tensor_scalar(t8(1), t8(0), -2.0, None, ALU.mult))
        pool(lambda e: e.tensor_tensor(t8(1), ltb, t8(1), ALU.add))
        pool(lambda e: e.memset(t8(2), 2.718281828459045))
        pool(lambda e: e.tensor_tensor(t8(3), t8(2), t8(1), ALU.pow))
        pool(lambda e: e.tensor_scalar(t8(3), t8(3), 1.0, None, ALU.add))
        need("act", ("cp", chain[0] - 1))
        put("act", lambda e: e.activation(t8(4), t8(3), ACT.Ln), "ln", 0)
        need("pool", ("ln", 0))
        pool(lambda e: e.tensor_scalar(t8(5), t8(4), -1.0, None, ALU.mult))
        pool(lambda e: e.tensor_tensor(t8(5), t8(2), t8(5), ALU.pow))
        pool(lambda e: e.tensor_tensor(t8(5), t8(5), t8(3), ALU.mult))
        pool(lambda e: e.tensor_scalar(t8(5), t8(5), 1.0, None, ALU.subtract))
        pool(lambda e: e.tensor_tensor(t8(4), t8(4), t8(5), ALU.add))
        pool(lambda e: e.tensor_tensor(t8(4), t8(4), t8(0), ALU.add))
        pool(lambda e: e.tensor_scalar(t8(4), t8(4), 0.1, None, ALU.add))
        pool(lambda e: e.tensor_scalar(t8(6), taub, -1.0, None, ALU.mult))
        pool(lambda e: e.tensor_tensor(t8(6), taub, t8(6), ALU.subtract))
        pool(lambda e: e.tensor_scalar(t8(7), taub, 0.0, None, ALU.max))
        pool(lambda e: e.tensor_scalar(t8(7), t8(7), 2.0, None, ALU.mult))
        pool(lambda e: e.tensor_tensor(t8(7), t8(7), taub, ALU.subtract))
        pool(lambda e: e.tensor_scalar(t8(7), t8(7), 0.1, None, ALU.add))
        need("pool", ("w", 0))
        pool(lambda e: e.tensor_tensor(S0[:, :, :], S0[:, :, :],
                                       sscale.unsqueeze(1).broadcast_to([128, 2, S]), ALU.mult))
        pool(lambda e: e.tensor_copy(bcA, bvc.unsqueeze(2).broadcast_to([128, 2, 128])))
        pool(lambda e: e.tensor_copy(bcB, fbvc.unsqueeze(2).broadcast_to([128, 2, 128])))
        pool(lambda e: e.tensor_copy(bcS, bshc.broadcast_to([64, 128])))
        setup_pool = ("cp", chain[0] - 1)

        dch = [0]

        def dve(fn):
            if dch[0]:
                need("dve", ("cd", dch[0] - 1))
            put("dve", fn, "cd", dch[0])
            dch[0] += 1

        need("dve", setup_pool, ("w", 0))
        dve(lambda e: e.reciprocal(t8(8), t8(4)))
        dve(lambda e: e.tensor_scalar(U[:, :], U[:, :], tmp8[0:64, 8:9], None, ALU.mult))
        dve(lambda e: e.reciprocal(t8(9), t8(7)))
        dve(lambda e: e.tensor_scalar(w2[:, :], w2[:, :], t8(9), None, ALU.mult))
        dve(lambda e: e.tensor_scalar(b2[:, :], b2raw, t8(9), None, ALU.mult))
        for c in range(2):
            dve(lambda e, c=c: e.tensor_scalar(wc[:, c, :], wc[:, c, :], wcs[:, c:c + 1], None, ALU.mult))
        dve(lambda e: e.tensor_scalar(wc[0:64, 2, :], wc[0:64, 2, :], wcs[0:64, 2:3], None, ALU.mult))
        dve(lambda e: e.tensor_reduce(mslot, S0[:, :, :], AX.X, ALU.add))
        dve(lambda e: e.tensor_scalar(mslot, mslot, 1.0 / S, None, ALU.mult))
        setup_dve = ("cd", dch[0] - 1)
        dve(lambda e: e.tensor_scalar(tg[:, 0, 0, 0:R], rbB, 1.0 / TWO_PI, MAGIC, ALU.mult, ALU.add))
        dve(lambda e: e.tensor_scalar(tg[:, 0, 0, 0:R], tg[:, 0, 0, 0:R], MAGIC, None, ALU.subtract))
        dve(lambda e: e.scalar_tensor_tensor(tg[:, 0, 1, 0:R], tg[:, 0, 0, 0:R], -PI_HI, rbB, ALU.mult, ALU.add))
        dve(lambda e: e.scalar_tensor_tensor(biasC[:, 1, :], tg[:, 0, 0, 0:R], -PI_LO, tg[:, 0, 1, 0:R],
                                             ALU.mult, ALU.add))
        dve(lambda e: e.tensor_scalar(biasC[:, 0, :], biasC[:, 1, :], TWO_PI / 4, None, ALU.add))
        dve(lambda e: e.tensor_tensor(bhh[:, 0:4], bhh[:, 0:4], bihn[:, 0:4], ALU.add))

        def setup_mm(w, steps, evac, extra=None):
            i, p = G.take()
            for s, (l, r) in enumerate(steps):
                last = s == len(steps) - 1
                m, n = l.shape[-1], r.shape[-1]
                fn = lambda e, p=p, l=l, r=r, s=s, last=last, m=m, n=n: e.matmul(
                    p[0:m, 0:n], l, r, start=s == 0, stop=last)
                if last:
                    put("pe", fn, "sm", q.counts.get("sm", 0))
                else:
                    put("pe", fn)
            need("dve", ("sm", q.counts["sm"] - 1))
            dve(lambda e, p=p: evac(e, p))
            G.freed[i] = ("cd", dch[0] - 1)

        need("pe", setup_pool, setup_dve, ("w", 0))
        for c in range(2):
            cs = slice(c * 128, c * 128 + 128)
            setup_mm(D, [(wv_n[:, k, cs], woT[:, k, :]) for k in range(2)],
                     lambda e, p, c=c: e.tensor_copy(W1[:, c, 0:256], p[:, 0:256]))
            setup_mm(R, [(wsh[:, cs], omT)], lambda e, p, c=c: e.tensor_copy(W1[:, c, 321:353], p[:, 0:R]))
            setup_mm(D, [(fwv[:, k, cs], fwoT[:, k, :]) for k in range(2)],
                     lambda e, p, c=c: e.tensor_copy(Wvo[:, c, :], p[:, 0:256]))
        setup_mm(D, [(bcA[:, k, :], woT[:, k, :]) for k in range(2)] + [(ones[0:1, :], boutr)],
                 lambda e, p: e.tensor_copy(biasM[:, 0:256], p[:, 0:256]))
        setup_mm(D, [(bcB[:, k, :], fwoT[:, k, :]) for k in range(2)] + [(ones[0:1, :], fbor)],
                 lambda e, p: e.tensor_copy(bSV[:, :], p[:, 0:256]))
        setup_mm(R, [(bcS, omT)], lambda e, p: e.tensor_copy(biasM[:, 321:353], p[:, 0:R]))
        setup_mm(64, [(ones[0:1, :], brow[:, 0:64])], lambda e, p: e.tensor_copy(biasM[:, 256:320], p[:, 0:64]))
        setup_mm(1, [(ones[0:1, :], brow[:, 64:65])], lambda e, p: e.tensor_copy(biasM[:, 320:321], p[:, 0:1]))
        setup_mm(1, [(w1b[:, k, :], mslot[:, k:k + 1]) for k in range(2)],
                 lambda e, p: e.tensor_tensor(b1[:, :], b1[:, :], p[:, 0:1], ALU.add))
        for j in range(6):
            setup_mm(S, [(whh[:, k, j * 128:j * 128 + 128], S0[:, k, :]) for k in range(2)],
                     lambda e, p, j=j: e.tensor_scalar(GH[:, j, :], p[:, 0:S], bhh[:, j:j + 1], None, ALU.add))
        dve(lambda e: e.tensor_scalar(HN[:, :, :], GH[:, 4:6, :], 0.5, None, ALU.mult))
        ready = ("cd", dch[0] - 1)
        for eng in ("pe", "act", "pool"):
            need(eng, ready)

        def norm(src, src_p, b, st, m, r, dst, tag, war):
            d = b % 2
            need("dve", src_p, (tag + "_n", b - 2))
            for t in range(4):
                put("dve", lambda e, t=t: e.bn_stats(st[:, d, t, :], src[:, t, :]), tag + "_s", 4 * b + t)
            for t in range(4):
                need("dve", (tag + "_s", 4 * b + t))
                put("dve", lambda e, t=t: e.bn_aggr(m[:, d, t, :], st[:, d, t, :]), tag + "_a", 4 * b + t)
            need("pool", (tag + "_a", 4 * b + 3), src_p)
            put("pool", lambda e: e.tensor_scalar(r[:, d, 1, :], m[:, d, :, 1], 1e-5, None, ALU.add), tag + "_v", b)
            need("pool", (tag + "_v", b))
            put("pool", lambda e: e.tensor_tensor(r[:, d, 0, :], r[:, d, 1, :], half[:, 0:4], ALU.pow), tag + "_r", b)
            need("pool", (tag + "_r", b))
            put("pool", lambda e: e.tensor_tensor(r[:, d, 1, :], m[:, d, :, 0], r[:, d, 0, :], ALU.mult),
                tag + "_m", b)
            need("pool", (tag + "_m", b))
            put("pool", lambda e: e.tensor_scalar(r[:, d, 2, :], r[:, d, 1, :], -1.0, None, ALU.mult), tag + "_m2", b)
            need("pool", (tag + "_m2", b), *war)
            for t in range(4):
                put("pool", lambda e, t=t: e.tensor_scalar(dst[:, t, :], src[:, t, :], r[:, d, 0, t:t + 1],
                                                           r[:, d, 2, t:t + 1], ALU.mult, ALU.add),
                    *((tag + "_n", b) if t == 3 else ()))

        def transposed(srcs, p_src, width, evac_eng, evac, name, n):
            i, p = T.take()
            need("pe", *p_src)
            for j, s in enumerate(srcs):
                m = s.shape[-1]
                fn = lambda e, j=j, s=s, m=m, p=p: e.transpose(p[0:m, j * 128:j * 128 + 128], s, ident[:, :])
                put("pe", fn, *((name + "_t", n) if j == len(srcs) - 1 else ()))
            need(evac_eng, (name + "_t", n))
            put(evac_eng, lambda e, p=p: evac(e, p), name, n)
            T.freed[i] = (name, n)

        def front(k):
            bs = (2 * k, 2 * k + 1)
            for b in bs:
                norm(X[:, b % NX, :, :], ("x", b), b, stats, mv, rs, xn[:, b % 2, :, :], "ln", [("xnT", 2 * (b - 2) + 1)])
            yield
            for b in bs:
                d = b % 2
                for c in range(2):
                    need("act", ("vs_mm", 4 * (b - 2) + 3))
                    transposed([xn[:, d, t, c * 128:c * 128 + 128] for t in range(4)], [("ln_n", b)], 512, "act",
                               lambda e, p, c=c, d=d: e.activation(xnT[:, d, c, :], p[:, :], ACT.Copy),
                               "xnT", 2 * b + c)
                yield
            for b in bs:
                d = b % 2
                for t in range(4):
                    i, p = G.take()
                    need("pe", ("xnT", 2 * b + 1))
                    for c in range(2):
                        put("pe", lambda e, c=c, t=t, p=p, d=d: e.matmul(
                            p[:, 0:FEATS], xnT[:, d, c, t * 128:t * 128 + 128], W1[:, c, :],
                            start=c == 0, stop=c == 1), *(("vs_mm", 4 * b + t) if c else ()))
                    need("dve", ("vs_mm", 4 * b + t), ("av", 4 * (b - 4) + 3), ("trig", b // 2 - 2), ("q2", b // 2 - 2))
                    put("dve", lambda e, t=t, p=p, b=b: e.tensor_tensor(VS[:, b % 4, t, :], p[:, 0:FEATS],
                                                                       biasM[:, :], ALU.add), "vs", 4 * b + t)
                    G.freed[i] = ("vs", 4 * b + t)
                    if t == 1:
                        yield
                yield
            v0 = (2 * k) % 4
            VP = VS[:, v0:v0 + 2, :, :]
            need("act", ("vs", 4 * bs[1] + 3), ("tp", bs[1] - 2))
            put("act", lambda e: e.activation(qq[:, :, :, 0:1], VP[:, :, :, 320:321], ACT.Tanh), "q1", k)
            for b in bs:
                d = b % 2
                need("dve", ("vs", 4 * b + 3), ("sin", k - 1))
                put("dve", lambda e, b=b, d=d: e.tensor_tensor(tg[:, d, :, :], VS[:, b % 4, :, 256:320],
                                                              VS[:, b % 4, :, 256:320], ALU.mult), "sq", b)
                need("dve", ("sq", b))
                put("dve", lambda e, d=d: e.tensor_reduce(n2[:, d, 0, :], tg[:, d, :, :], AX.X, ALU.add), "n2", b)
            need("pool", ("n2", bs[1]))
            put("pool", lambda e: e.tensor_scalar(n2[:, :, 1, :], n2[:, :, 0, :], 1e-24, None, ALU.max), "n2m", k)
            need("pool", ("n2m", k))
            put("pool", lambda e: e.tensor_tensor(n2[:, :, 0, :], n2[:, :, 1, :],
                                                  half[:, :].rearrange("p (a b) -> p a b", a=2), ALU.pow), "rn", k)
            need("pool", ("q1", k))
            put("pool", lambda e: e.tensor_tensor(qq[:, :, :, 1:2], qq[:, :, :, 0:1], qq[:, :, :, 0:1], ALU.mult),
                "q2", k)
            need("pool", ("q2", k))
            put("pool", lambda e: e.tensor_tensor(qq[:, :, :, 2:4], qq[:, :, :, 0:2],
                                                  qq[:, :, :, 1:2].broadcast_to([128, 2, 4, 2]), ALU.mult), "q4", k)
            yield
            for b in bs:
                d = b % 2
                need("dve", ("rn", k))
                put("dve", lambda e, b=b, d=d: e.tensor_tensor(
                    tg2[:, d, :, 0:R], VS[:, b % 4, :, 321:353],
                    n2[:, d, 0, :].unsqueeze(2).broadcast_to([128, 4, R]), ALU.mult), "p1", b)
                need("dve", ("p1", b))
                put("dve", lambda e, d=d: e.tensor_tensor(
                    tg[:, d, :, :].rearrange("p t (a r) -> p t a r", a=2),
                    tg2[:, d, :, 0:R].unsqueeze(2).broadcast_to([128, 4, 2, R]),
                    biasC[:, :, :].unsqueeze(1).broadcast_to([128, 4, 2, R]), ALU.add), "p2", b)
            f = lambda z: z[:, :, :, :].rearrange("p d t r -> p (d t r)")
            steps = [
                lambda e: e.tensor_scalar(f(tg2), f(tg), 1.0 / TWO_PI, MAGIC, ALU.mult, ALU.add),
                lambda e: e.tensor_scalar(f(tg2), f(tg2), MAGIC, None, ALU.subtract),
                lambda e: e.scalar_tensor_tensor(f(tg), f(tg2), -PI_HI, f(tg), ALU.mult, ALU.add),
                lambda e: e.scalar_tensor_tensor(f(tg), f(tg2), -PI_LO, f(tg), ALU.mult, ALU.add),
                lambda e: e.tensor_scalar(f(tg), f(tg), PI_CLAMP, -PI_CLAMP, ALU.min, ALU.max),
            ]
            need("dve", ("p2", bs[1]))
            for j, s in enumerate(steps):
                put("dve", s, *(("p3", 5 * k + j) if j < 4 else ("trig", k)))
                if j < 4:
                    need("dve", ("p3", 5 * k + j))
            yield
            for b in bs:
                d = b % 2
                need("act", ("trig", k), ("tp", b - 2))
                if b == bs[0]:
                    put("act", lambda e: e.activation(f(tg2), f(tg), ACT.Sin), "sin", k)
            for b in bs:
                d = b % 2
                need("pool", ("sin", k), ("q4", k), ("tpT_t", 3 * (b - 1) + 2))
                put("pool", lambda e, d=d: e.tensor_copy(tp[:, 0, :, 0, :], tg2[:, d, :, :]))
                put("pool", lambda e, d=d: e.tensor_tensor(
                    tp[:, 0, :, 1:5, :], tg2[:, d, :, :].unsqueeze(2).broadcast_to([128, 4, 4, 64]),
                    qq[:, d, :, :].unsqueeze(3).broadcast_to([128, 4, 4, 64]), ALU.mult), "tp", b)
                yield
                for j in range(3):
                    w = 128 if j < 2 else 64
                    need("act", ("phi", b - 1))
                    tv = tp[:, 0, :, :, :].rearrange("p t m r -> p t (m r)")
                    transposed([tv[:, t, j * 128:j * 128 + w] for t in range(4)], [("tp", b)], 512, "act",
                               lambda e, p, j=j, w=w: e.activation(tpT[0:w, 0, j, :], p[0:w, :], ACT.Copy),
                               "tpT", 3 * b + j)
                yield
                i, p = G.take()
                for j in range(3):
                    w = 128 if j < 2 else 64
                    need("pe", ("tpT", 3 * b + j))
                    put("pe", lambda e, j=j, w=w, p=p: e.matmul(p[0:C, :], wc[0:w, j, :], tpT[0:w, 0, j, :],
                                                              start=j == 0, stop=j == 2),
                        *(("phi", b) if j == 2 else ()))
                need("dve", ("phi", b), ("lg_mm", 4 * (b - 4) + 3))
                put("dve", lambda e, p=p, b=b: e.tensor_tensor(QT[:, b % 4, :], p[0:C, :], U[:, :], ALU.mult),
                    "QT", b)
                put("dve", lambda e, p=p, b=b: e.tensor_tensor(KT[:, b % 4, :], p[0:C, :], Wk[:, :], ALU.mult),
                    "KT", b)
                G.freed[i] = ("KT", b)
                yield

        def attn(k):
            rows = [(b, i) for b in (2 * k, 2 * k + 1) for i in range(4)]

            def logits(b, i):
                r = 4 * b + i
                w = (i + 1) * 128
                bi, p = L.take()
                need("pe", ("KT", b))
                put("pe", lambda e: e.matmul(p[:, 0:w], QT[:, b % 4, i * 128:w], KT[:, b % 4, 0:w],
                                             start=True, stop=False, skip_group_check=True))
                put("pe", lambda e: e.matmul(p[:, i * 128:w], identb[:, :], maskb[:, :], start=False, stop=True,
                                             skip_group_check=True), "lg_mm", r)
                need("dve", ("lg_mm", r), ("E", r - 8))
                put("dve", lambda e: e.tensor_reduce(nmax[:, r % 8:r % 8 + 1], p[:, 0:w], AX.X, ALU.max,
                                                     negate=True), "nmax", r)
                need("act", ("nmax", r), ("ET_t", r - 2), ("av", r - 8))
                put("act", lambda e: e.activation(E[:, r % 2, 0:w], p[:, 0:w], ACT.Exp,
                                                  bias=nmax[:, r % 8:r % 8 + 1],
                                                  accum_out=rsum[:, r % 8:r % 8 + 1]), "E", r)
                L.freed[bi] = ("E", r)
                need("dve", ("E", r))

            def probs(b, i):
                r = 4 * b + i
                w = (i + 1) * 128
                need("act", ("av_mm", r - 2))
                transposed([E[:, r % 2, j * 128:j * 128 + 128] for j in range(i + 1)], [("E", r)], w, "act",
                           lambda e, p: e.activation(ET[:, r % 2, 0:w], p[:, 0:w], ACT.Copy), "ET", r)

            def values(b, i):
                r = 4 * b + i
                bi, p = O.take()
                need("pe", ("ET", r), ("vs", 4 * b + 3))
                for j in range(i + 1):
                    put("pe", lambda e, j=j: e.matmul(p[:, 0:D], ET[:, r % 2, j * 128:j * 128 + 128],
                                                      VS[:, b % 4, j, 0:256], start=j == 0, stop=j == i),
                        *(("av_mm", r) if j == i else ()))
                need("dve", ("E", r))
                put("dve", lambda e: e.reciprocal(rinv[:, r % 8:r % 8 + 1], rsum[:, r % 8:r % 8 + 1]), "rinv", r)
                need("dve", ("av_mm", r), ("rinv", r), ("st", b - NY))
                put("dve", lambda e: e.scalar_tensor_tensor(
                    x1[:, b % NY, i, :], p[:, 0:D], rinv[:, r % 8:r % 8 + 1], X[:, b % NX, i, :],
                    ALU.mult, ALU.add), "av", r)
                O.freed[bi] = ("av", r)
                if i == 3:
                    q.at[("x1", b)] = q.at[("av", r)]

            for n in range(len(rows) + 2):
                if n < len(rows):
                    logits(*rows[n])
                if 1 <= n <= len(rows):
                    probs(*rows[n - 1])
                if n >= 2:
                    values(*rows[n - 2])
                yield

        def back(k):
            bs = (2 * k, 2 * k + 1)
            for b in bs:
                norm(x1[:, b % NY, :, :], ("x1", b), b, stats2, mv2, rs2, xm[:, b % 2, :, :], "lm",
                     [("xmT", 2 * (b - 2) + 1), ("gi_mm", b - 2)])
            yield
            for b in bs:
                d = b % 2
                for c in range(2):
                    need("act", ("h_mm", b - 1))
                    transposed([xm[:, d, t, c * 128:c * 128 + 128] for t in range(4)], [("lm_n", b)], 512, "act",
                               lambda e, p, c=c: e.activation(xmT[:, 0, c, :], p[:, :], ACT.Copy),
                               "xmT", 2 * b + c)
                yield
                i, p = G.take()
                need("pe", ("xmT", 2 * b + 1))
                for c in range(2):
                    put("pe", lambda e, c=c, p=p: e.matmul(p[:, :], w1a[:, c, :], xmT[:, 0, c, :],
                                                         start=c == 0, stop=c == 1),
                        *(("h_mm", b) if c else ()))
                G.freed[i] = ("h", b)
                need("act", ("h_mm", b), ("rt_mm", b - 2))
                put("act", lambda e, p=p, d=d: e.activation(hT[:, d, :], p[:, :], ACT.Gelu, bias=b1[:, 0:1]), "h", b)
                yield
            for b in bs:
                d = b % 2
                i, p = G.take()
                need("pe", ("h", b))
                for t in range(4):
                    put("pe", lambda e, t=t, p=p, d=d: e.matmul(p[:, t * S:t * S + S], hT[:, d, t * 128:t * 128 + 128],
                                                              w2[:, :], start=True, stop=True, skip_group_check=True),
                        *(("rt_mm", b) if t == 3 else ()))
                need("dve", ("rt_mm", b), ("dm", b - 2))
                put("dve", lambda e, p=p, d=d: e.tensor_tensor(
                    lg[:, d, 0, :, :], p[:, 0:4 * S].rearrange("p (t s) -> p t s", t=4),
                    b2[:, :].unsqueeze(1).broadcast_to([128, 4, S]), ALU.add), "lg", b)
                G.freed[i] = ("lg", b)
                need("dve", ("lg", b))
                for t in range(4):
                    put("dve", lambda e, t=t, d=d: e.max(m8[:, d, t, :], lg[:, d, 0, t, :]), "m8", 4 * b + t)
                for t in range(4):
                    need("dve", ("m8", 4 * b + t))
                    put("dve", lambda e, t=t, d=d: e.match_replace(lg[:, d, 1, t, :], m8[:, d, t, :],
                                                                  lg[:, d, 0, t, :], -3e38), "mr", 4 * b + t)
                need("pool", ("mr", 4 * b + 3), ("ex", b - 2))
                for z in range(2):
                    put("pool", lambda e, d=d, z=z: e.tensor_tensor(
                        lg[:, d, z, :, :], lg[:, d, z, :, :],
                        m8[:, d, :, 0:1].broadcast_to([128, 4, S]), ALU.subtract), *(("dm", b) if z else ()))
                yield
            for b in bs:
                d = b % 2
                need("act", ("dm", b), ("am", b - 2))
                put("act", lambda e, d=d: e.activation(ex[:, d, :, :, :], lg[:, d, :, :, :], ACT.Exp), "ex", b)
                need("pool", ("ex", b))
                put("pool", lambda e, d=d: e.tensor_tensor(ex[:, d, 0, :, :], ex[:, d, 0, :, :], ex[:, d, 1, :, :],
                                                          ALU.subtract), "am0", b)
                need("dve", ("am0", b))
                put("dve", lambda e, d=d: e.tensor_reduce(asum[:, d, 0, :], ex[:, d, 0, :, :], AX.X, ALU.add),
                    "as0", b)
                need("dve", ("as0", b))
                put("dve", lambda e, d=d: e.reciprocal(asum[:, d, 1, :], asum[:, d, 0, :]), "as1", b)
                need("pool", ("as1", b), ("aT_t", k - 2), ("gi_mm", b - 4))
                put("pool", lambda e, d=d: e.tensor_tensor(
                    AL[:, k % 2, :, d, :], ex[:, d, 0, :, :],
                    asum[:, d, 1, :].unsqueeze(2).broadcast_to([128, 4, S]), ALU.mult), "am", b)
                need("pool", ("am", b), ("gi_mm", b - 2))
                put("pool", lambda e, d=d: e.tensor_tensor(ex[:, d, 1, 0:2, :], AL[:, k % 2, 0:2, d, :],
                                                          AL[:, k % 2, 2:4, d, :], ALU.add), "al0", b)
                need("pool", ("al0", b))
                put("pool", lambda e, d=d: e.tensor_tensor(alt[:, d, :], ex[:, d, 1, 0, :], ex[:, d, 1, 1, :],
                                                          ALU.add), "al", b)
                yield
            for b in bs:
                d = b % 2
                i, p = G.take()
                need("pe", ("am", b), ("al", b), ("lm_n", b))
                for c in range(2):
                    for t in range(4):
                        put("pe", lambda e, c=c, t=t, p=p, d=d: e.matmul(
                            p[:, c * S:c * S + S], xm[:, d, t, c * 128:c * 128 + 128], AL[:, k % 2, t, d, :],
                            start=t == 0, stop=t == 3))
                put("pe", lambda e, p=p, d=d: e.matmul(p[:, 2 * S:3 * S], ones[:, :], alt[:, d, :],
                                                     start=True, stop=True), "gi_mm", b)
                need("dve", ("gi_mm", b), ("gi", b - 1))
                put("dve", lambda e, p=p: e.tensor_scalar(rw[:, :], p[:, 2 * S:3 * S], 1e-8, None, ALU.add), "rw0", b)
                need("dve", ("rw0", b))
                put("dve", lambda e: e.reciprocal(rw[:, :], rw[:, :]), "rw", b)
                need("dve", ("rw", b), ("gx_mm", k - 2))
                put("dve", lambda e, p=p, d=d: e.tensor_tensor(
                    GI[:, k % 2, :, d, :], p[:, 0:2 * S].rearrange("p (c s) -> p c s", c=2),
                    rw[:, :].unsqueeze(1).broadcast_to([128, 2, S]), ALU.mult), "gi", b)
                G.freed[i] = ("gi", b)
                yield

        def slots(k):
            i1, p1 = G.take()
            need("pe", ("gi", 2 * k + 1))
            gx = lambda j, c: (wih[:, c, j * 128:j * 128 + 128], GI[:, k % 2, c, :, :].rearrange("p b s -> p (b s)"))
            for j in range(4):
                for c in range(2):
                    put("pe", lambda e, j=j, c=c: e.matmul(p1[:, j * 128:j * 128 + 128], *gx(j, c),
                                                           start=c == 0, stop=c == 1),
                        *(("rz_mm", k) if j == 3 and c else ()))
            need("dve", ("rz_mm", k))
            put("dve", lambda e: e.tensor_tensor(
                grz[:, :, :, :], p1[:, :].rearrange("p (j b s) -> p j b s", j=4, b=2),
                GH[:, 0:4, :].unsqueeze(2).broadcast_to([128, 4, 2, S]), ALU.add), "grz", k)
            G.freed[i1] = ("grz", k)
            yield
            i2, p2 = G.take()
            for j in range(2):
                for c in range(2):
                    put("pe", lambda e, j=j, c=c: e.matmul(p2[:, j * 128:j * 128 + 128], *gx(4 + j, c),
                                                           start=c == 0, stop=c == 1),
                        *(("gx_mm", k) if j and c else ()))
            need("act", ("grz", k))
            fl = lambda z: z.rearrange("p c b s -> p (c b s)")
            put("act", lambda e: e.activation(fl(grz[:, :, :, :]), fl(grz[:, :, :, :]), ACT.Tanh, scale=0.5), "srz", k)
            need("dve", ("srz", k))
            put("dve", lambda e: e.scalar_tensor_tensor(
                gt[:, 0, :, :], grz[:, 0, :, :], 1.0,
                HN[:, 0, :].unsqueeze(1).broadcast_to([128, 2, S]), ALU.add, ALU.mult))
            put("dve", lambda e: e.scalar_tensor_tensor(
                gt[:, 1, :, :], grz[:, 1, :, :], 1.0,
                HN[:, 1, :].unsqueeze(1).broadcast_to([128, 2, S]), ALU.add, ALU.mult), "rhn", k)
            need("dve", ("rhn", k), ("gx_mm", k))
            put("dve", lambda e: e.tensor_tensor(fl(gn[:, :, :, :]), p2[:, 0:256], fl(gt[:, :, :, :]), ALU.add),
                "gn", k)
            G.freed[i2] = ("gn", k)
            need("act", ("gn", k))
            for c in range(2):
                put("act", lambda e, c=c: e.activation(gn[:, c, :, :], gn[:, c, :, :], ACT.Tanh,
                                                       bias=bihn[:, 4 + c:5 + c]), *(("nn", k) if c else ()))
            yield
            need("pool", ("nn", k))
            put("pool", lambda e: e.tensor_tensor(
                gt[:, :, :, :], S0[:, :, :].unsqueeze(2).broadcast_to([128, 2, 2, S]), gn[:, :, :, :],
                ALU.subtract), "hd", k)
            need("dve", ("hd", k))
            put("dve", lambda e: e.scalar_tensor_tensor(fl(gt[:, :, :, :]), fl(grz[:, 2:4, :, :]), 1.0,
                                                        fl(gt[:, :, :, :]), ALU.add, ALU.mult), "hz", k)
            need("dve", ("hz", k), ("sv_mm", k - 1))
            put("dve", lambda e: e.scalar_tensor_tensor(fl(SN[:, :, :, :]), fl(gt[:, :, :, :]), 0.5,
                                                        fl(gn[:, :, :, :]), ALU.mult, ALU.add), "sn", k)
            need("act", ("of_mm", 8 * (k - 2) + 7))
            transposed([AL[:, k % 2, t, :, :].rearrange("p b s -> p (b s)") for t in range(4)],
                       [("am", 2 * k + 1)], 512, "act",
                       lambda e, p: e.activation(aT[:, k % 2, :], p[:, :], ACT.Copy), "aT", k)
            yield
            i3, p3 = G.take()
            need("pe", ("sn", k))
            for c in range(2):
                put("pe", lambda e, c=c: e.matmul(p3[:, 0:D], SN[:, c, :, :].rearrange("p b s -> p (b s)"),
                                                  Wvo[:, c, :], start=c == 0, stop=c == 1),
                    *(("sv_mm", k) if c else ()))
            need("dve", ("sv_mm", k), ("of_mm", 8 * (k - 2) + 7))
            put("dve", lambda e: e.tensor_tensor(SV[:, k % 2, :], p3[:, 0:D], bSV[:, :], ALU.add), "sv", k)
            G.freed[i3] = ("sv", k)
            yield
            for b in (2 * k, 2 * k + 1):
                h = slice(64 * (b % 2), 64 * (b % 2) + 64)
                for t in range(4):
                    bi, p = O.take()
                    need("pe", ("aT", k), ("sv", k))
                    put("pe", lambda e, t=t, p=p, h=h: e.matmul(p[:, 0:D], aT[h, k % 2, t * 128:t * 128 + 128],
                                                              SV[h, k % 2, :], start=True, stop=True),
                        "of_mm", 4 * b + t)
                    need("dve", ("of_mm", 4 * b + t), ("lm_n", b))
                    put("dve", lambda e, t=t, p=p, b=b: e.tensor_tensor(x1[:, b % NY, t, :], p[:, 0:D],
                                                                       x1[:, b % NY, t, :], ALU.add), "fin", 4 * b + t)
                    O.freed[bi] = ("fin", 4 * b + t)
                    if t == 1:
                        yield
                need("sp", ("fin", 4 * b + 3))
                put("sp", lambda e, b=b: e.dma_start(out[b].rearrange("(t p) d -> p t d", p=128), x1[:, b % NY, :, :]),
                    "st", b, sem=f"st{b % NY}", by=16)
                yield

        NP = B // 2
        for it in range(NP + 3):
            gens = {}
            if it < NP:
                gens["F"] = front(it)
            if 0 <= it - 1 < NP:
                gens["A"] = attn(it - 1)
            if 0 <= it - 2 < NP:
                gens["B"] = back(it - 2)
            if 0 <= it - 3 < NP:
                gens["S"] = slots(it - 3)
            for c in ORDERING:
                g = gens.get(c)
                if g is not None:
                    next(g, None)
            for g in gens.values():
                for _ in g:
                    pass
            for b in (2 * it + 4, 2 * it + 5):
                if b < B:
                    load_x(b)
        need("sp", *[("st", b) for b in range(B)])

        block = ctx.enter_context(nc.Block())

        @block.sync
        def _(e):
            for fn in q.lists["sp"]:
                fn(e)

        @block.gpsimd
        def _(e):
            for fn in q.lists["pool"]:
                fn(e)

        @block.scalar
        def _(e):
            for fn in q.lists["act"]:
                fn(e)

        @block.vector
        def _(e):
            for fn in q.lists["dve"]:
                fn(e)

        @block.tensor
        def _(e):
            for fn in q.lists["pe"]:
                fn(e)


ORDERING = "FBAS" * 12


def kernel(**inputs):
    import concourse.bacc as bacc
    from concourse.bass_utils import run_bass_kernel_spmd

    g = {k: np.asarray(v) for k, v in inputs.items()}
    at, ff = "L0_attn_", "L0_ffn_"
    con = np.ascontiguousarray
    ramp = np.arange(N, dtype=np.float64) - (N - 1) / 2
    arrays = {
        "x": g[at + "x"],
        "b_charge": g[at + "b_charge"],
        "W_shell": g[at + "W_shell"],
        "W_scT": con(np.concatenate([g[at + "W_shell"], g[at + "W_charge"]]).T),
        "b_shell": g[at + "b_shell"],
        "omegaT": con(g[at + "omega"].T),
        "rff_bias": g[at + "rff_bias"],
        "W_combineT": con(g[at + "W_combine"].T),
        "W_v": g[at + "W_v"],
        "b_v": con(g[at + "b_v"].reshape(2, 128).T),
        "W_outT": con(g[at + "W_out"].T),
        "b_out": g[at + "b_out"],
        "log_temp": con(g[at + "log_temp"].reshape(1)),
        "decay": np.stack([np.exp(-0.03 * ramp), np.exp(0.03 * ramp)]).astype(np.float32),
        "slot_initT": con(g[ff + "slot_init"].T),
        "slot_scale": con(g[ff + "slot_scale"].reshape(-1)),
        "w1T": con(g[ff + "w1"].T),
        "b1": g[ff + "b1"],
        "w2T": con(g[ff + "w2"].T),
        "b2": g[ff + "b2"],
        "gru_wihT": con(g[ff + "gru_wih"].T),
        "gru_whhT": con(g[ff + "gru_whh"].T),
        "gru_bih": con(g[ff + "gru_bih"].reshape(6, 128).T),
        "gru_bhh": con(g[ff + "gru_bhh"].reshape(6, 128).T),
        "wv": g[ff + "wv"],
        "bv": con(g[ff + "bv"].reshape(2, 128).T),
        "woT": con(g[ff + "wo"].T),
        "bo": g[ff + "bo"],
        "tau": g[ff + "tau"],
    }
    nc = bacc.Bacc("TRN2", target_bir_lowering=False, num_devices=1)
    aps = {k: nc.dram_tensor("in_" + k, v.shape, mybir.dt.from_np(v.dtype), kind="ExternalInput").ap()
           for k, v in arrays.items()}
    out = nc.dram_tensor("out_x", (B, N, D), FP, kind="ExternalOutput").ap()
    build(nc, aps, out)
    r = run_bass_kernel_spmd(nc, [{"in_" + k: v for k, v in arrays.items()}], core_ids=[0])
    return r.results[0]["out_x"]
```

```python
import numpy as np
import concourse.bass as bass
from concourse import mybir
from contextlib import ExitStack

B, N, D = 32, 512, 256
S, H, R, C = 64, 128, 32, 64
ORDER = 4
FP = mybir.dt.float32
BF = mybir.dt.bfloat16
FR = mybir.dt.float32r
ALU = mybir.AluOpType
ACT = mybir.ActivationFunctionType
AX = mybir.AxisListType
MAGIC = 12582912.0
TWO_PI = 6.283185307179586
PI_HI = 6.28125
PI_LO = TWO_PI - PI_HI
PI_CLAMP = 3.1415925
FEATS = 354


class Queues:

    def __init__(self, nc, ctx):
        self.nc, self.ctx = nc, ctx
        self.lists = {k: [] for k in ("pe", "act", "dve", "pool", "sp")}
        self.sems, self.counts, self.at, self.seen = {}, {}, {}, {}

    def sem(self, name):
        if name not in self.sems:
            self.sems[name] = self.ctx.enter_context(self.nc.semaphore("s_" + name))
            self.counts[name] = 0
        return self.sems[name]

    def need(self, eng, *products):
        for name, n in products:
            if n < 0:
                continue
            sem, value = self.at[(name, n)]
            if self.seen.get((eng, sem), 0) >= value:
                continue
            self.seen[(eng, sem)] = value
            s = self.sems[sem]
            self.lists[eng].append(lambda e, s=s, v=value: e.wait_ge(s, v))

    def put(self, eng, fn, name=None, n=0, sem=None, by=1):
        if name is None:
            self.lists[eng].append(fn)
            return
        sem = sem or name
        s = self.sem(sem)
        self.counts[sem] += by
        self.at[(name, n)] = (sem, self.counts[sem])
        self.lists[eng].append(lambda e: fn(e).then_inc(s, by))


class Banks:

    def __init__(self, q, tensors):
        self.q, self.tensors, self.n = q, tensors, 0
        self.freed = [None] * len(tensors)

    def take(self):
        i = self.n % len(self.tensors)
        self.n += 1
        if self.n > len(self.tensors):
            assert self.freed[i] is not None, "taken again before its reader is queued"
            self.q.need("pe", self.freed[i])
        self.freed[i] = None
        return i, self.tensors[i]


def build(nc, a, out):
    ctx = ExitStack()
    with ctx:
        q = Queues(nc, ctx)
        need, put = q.need, q.put

        def sb(name, shape, dt=FP):
            return ctx.enter_context(nc.sbuf_tensor(name, shape, dt))

        banks = [ctx.enter_context(nc.psum_tensor(f"ps{i}", [128, 512], FP)) for i in range(8)]
        T = Banks(q, banks[0:2])
        L = Banks(q, banks[2:4])
        G = Banks(q, banks[4:7])
        O = Banks(q, banks[7:8])

        ident = sb("ident", [128, 128])
        identb = sb("identb", [128, 128], BF)
        maskb = sb("maskb", [128, 128], BF)
        ones = sb("ones", [128, 128])
        W1h = sb("W1h", [128, 2, FEATS], FR)
        W1l = sb("W1l", [128, 2, FEATS], FR)
        biasM = sb("biasM", [128, FEATS])
        biasC = sb("biasC", [128, 2, R])
        wc = sb("wc", [128, 3, C])
        wcs = sb("wcs", [128, 3])
        U = sb("U", [128, N])
        Wk = sb("Wk", [128, N])
        w1a = sb("w1a", [128, 2, H])
        b1 = sb("b1", [128, 1])
        w2 = sb("w2", [128, S])
        b2 = sb("b2", [128, S])
        wih = sb("wih", [128, 2, 3 * D])
        GH = sb("GH", [128, 6, S])
        HN = sb("HN", [128, 2, S])
        bihn = sb("bihn", [128, 6])
        S0 = sb("S0", [128, 2, S])
        Wvo = sb("Wvo", [128, 2, D])
        bSV = sb("bSV", [128, D])
        half = sb("half", [128, 8])

        NX = 6
        X = sb("X", [128, NX, 4, D])
        stats = sb("stats", [128, 2, 4, 6])
        mv = sb("mv", [128, 2, 4, 2])
        rs = sb("rs", [128, 2, 3, 4])
        xn = sb("xn", [128, 2, 4, D])
        xh = sb("xh", [128, 2, 2, N], FR)
        xl = sb("xl", [128, 2, 2, N], FR)
        VS = sb("VS", [128, 4, 4, FEATS])
        tg = sb("tg", [128, 2, 4, 2 * R])
        tg2 = sb("tg2", [128, 2, 4, 2 * R])
        qq = sb("qq", [128, 2, 4, 4])
        n2 = sb("n2", [128, 2, 2, 4])
        tp = sb("tp", [128, 2, 4, 5, 64])
        tpT2 = sb("tpT2", [64, 2, N])
        QT = sb("QT", [128, 2, N])
        KT = sb("KT", [128, 2, N])
        nmax = sb("nmax", [128, 8])
        rsum = sb("rsum", [128, 8])
        rinv = sb("rinv", [128, 8])
        E = sb("E", [128, 3, N])
        ET = sb("ET", [128, 2, N])
        NY = 6
        x1 = sb("x1", [128, NY, 4, D])
        stats2 = sb("stats2", [128, 2, 4, 6])
        mv2 = sb("mv2", [128, 2, 4, 2])
        rs2 = sb("rs2", [128, 2, 3, 4])
        xm = sb("xm", [128, 4, 4, D])
        xmT = sb("xmT", [128, 2, 2, N])
        hT = sb("hT", [128, 2, N])
        lg = sb("lg", [128, 2, 2, 4, S])
        m8 = sb("m8", [128, 2, 4, 8])
        asum = sb("asum", [128, 2, 2, 4])
        AL = sb("AL", [128, 2, 4, 2, S])
        alt = sb("alt", [128, 2, S])
        rw = sb("rw", [128, S])
        GI = sb("GI", [128, 2, 2, 2, S])
        grz = sb("grz", [128, 4, 2, S])
        gn = sb("gn", [128, 2, 2, S])
        gt = sb("gt", [128, 2, 2, S])
        SN = sb("SN", [128, 2, 2, S])
        SV = sb("SV", [128, 2, D])
        aT = sb("aT", [128, 2, N])

        def tpT(d, j):
            return xmT[:, d, j, :] if j < 2 else tpT2[:, d, :]

        wv_n = x1[:, 0, 0:2, :]
        woT = x1[:, 0, 2:4, :]
        fwv = x1[:, 1, 0:2, :]
        fwoT = x1[:, 1, 2:4, :]
        whh = x1[:, 2:4, :, :].rearrange("p a t d -> p (a t d)")[:, 0:2 * 3 * D].rearrange("p (c n) -> p c n", c=2)
        stg = x1[:, 4, :, :].rearrange("p t d -> p (t d)")
        bvc = stg[:, 0:2]
        boutr = stg[0:1, 8:8 + D]
        fbvc = stg[:, 2:4]
        fbor = stg[0:1, 264:264 + D]
        wsh = stg[0:64, 520:776]
        omT = stg[0:64, 776:808]
        bshc = stg[0:64, 808:809]
        brow = stg[0:1, 812:812 + 65]
        rbB = stg[:, 880:912]
        mslot = stg[:, 912:914]
        bhh = stg[:, 914:920]
        ltb = stg[:, 920:921]
        taub = stg[:, 921:922]
        tmp8 = stg[:, 922:938]
        stg2 = x1[:, 5, :, :].rearrange("p t d -> p (t d)")
        w1b = stg2[:, 0:2 * H].rearrange("p (c n) -> p c n", c=2)
        sscale = stg2[:, 256:320]
        bcA = stg2[:, 320:320 + 256].rearrange("p (c n) -> p c n", c=2)
        bcB = stg2[:, 576:576 + 256].rearrange("p (c n) -> p c n", c=2)
        bcS = stg2[0:64, 832:960]
        b2raw = stg2[:, 960:1024]
        W1 = VS[:, 3, 0:2, :]

        def load(dst, src, eng="sp"):
            put(eng, lambda e, d=dst, s=src: e.dma_start(d, s), "w" if eng == "sp" else "wf", 0, by=16)

        def loadf(dst, src):
            load(dst, src, "act")

        def chunks(ap, c=2):
            return ap.rearrange("(c p) n -> p c n", c=c)

        def load_x(b):
            need("sp", ("x1", b - NX))
            put("sp", lambda e, b=b: e.dma_start(X[:, b % NX, :, :], a["x"][b].rearrange("(t p) d -> p t d", p=128)),
                "x", b, sem=f"x{b % NX}", by=16)

        load_x(0)
        load_x(1)
        load(wv_n, chunks(a["W_v"]))
        load(woT, chunks(a["W_outT"]))
        load(wsh, a["W_shell"])
        load(omT, a["omegaT"])
        load(bshc, a["b_shell"].rearrange("(p a) -> p a", a=1))
        load(brow[:, 0:64], a["b_shell"].rearrange("(a n) -> a n", a=1))
        load(brow[:, 64:65], a["b_charge"].rearrange("(a n) -> a n", a=1))
        load(W1[:, :, 256:321], chunks(a["W_scT"]))
        load(bvc, a["b_v"])
        load(boutr, a["b_out"].rearrange("(a n) -> a n", a=1))
        load(rbB, a["rff_bias"].partition_broadcast(128))
        load(wc[:, 0:2, :], a["W_combineT"][0:256, :].rearrange("(c p) n -> p c n", c=2))
        load(wc[0:64, 2, :], a["W_combineT"][256:320, :])
        load(U[:, :], a["decay"][0, :].partition_broadcast(128))
        load(Wk[:, :], a["decay"][1, :].partition_broadcast(128))
        load(ltb, a["log_temp"].partition_broadcast(128))
        loadf(fwv, chunks(a["wv"]))
        loadf(fwoT, chunks(a["woT"]))
        loadf(fbvc, a["bv"])
        loadf(fbor, a["bo"].rearrange("(a n) -> a n", a=1))
        loadf(whh, chunks(a["gru_whhT"]))
        loadf(wih[:, :, :], chunks(a["gru_wihT"]))
        loadf(w1a[:, :, :], chunks(a["w1T"][0:256, :]))
        loadf(w1b, chunks(a["w1T"][256:512, :]))
        loadf(b1[:, :], a["b1"].rearrange("(p a) -> p a", a=1))
        loadf(w2[:, :], a["w2T"])
        loadf(b2raw, a["b2"].partition_broadcast(128))
        loadf(bihn[:, :], a["gru_bih"])
        loadf(bhh, a["gru_bhh"])
        loadf(S0[:, :, :], chunks(a["slot_initT"]))
        loadf(sscale, a["slot_scale"].partition_broadcast(128))
        loadf(taub, a["tau"].partition_broadcast(128))
        load_x(2)
        load_x(3)

        chain = [0]

        def pool(fn, last=None):
            if chain[0]:
                need("pool", ("cp", chain[0] - 1))
            put("pool", fn, "cp", chain[0])
            chain[0] += 1

        pool(lambda e: e.memset(ident[:, :], 0.0))
        pool(lambda e: e.affine_select(out=ident[:, :], in_=ident[:, :], compare_op=ALU.not_equal, fill=1.0,
                                       base=0, pattern=[[-1, 128]], channel_multiplier=1))
        pool(lambda e: e.memset(identb[:, :], 0.0))
        pool(lambda e: e.affine_select(out=identb[:, :], in_=identb[:, :], compare_op=ALU.not_equal, fill=1.0,
                                       base=0, pattern=[[-1, 128]], channel_multiplier=1))
        pool(lambda e: e.memset(maskb[:, :], 0.0))
        pool(lambda e: e.affine_select(out=maskb[:, :], in_=maskb[:, :], compare_op=ALU.is_ge, fill=-1e30,
                                       base=0, pattern=[[-1, 128]], channel_multiplier=1))
        pool(lambda e: e.memset(ones[:, :], 1.0))
        pool(lambda e: e.memset(half[:, :], -0.5))
        def stat(src, t, src_p, b, st, m, tag):
            d = b % 2
            need("dve", src_p, (tag + "_n", b - 2))
            put("dve", lambda e: e.bn_stats(st[:, d, t, :], src[:, t, :]), tag + "_s", 4 * b + t)
            need("dve", (tag + "_s", 4 * b + t))
            put("dve", lambda e: e.bn_aggr(m[:, d, t, :], st[:, d, t, :]), tag + "_a", 4 * b + t)

        def norm(src, src_p, b, m, r, dst, tag, war):
            d = b % 2
            need("pool", (tag + "_a", 4 * b + 3), src_p)
            put("pool", lambda e: e.tensor_scalar(r[:, d, 1, :], m[:, d, :, 1], 1e-5, None, ALU.add), tag + "_v", b)
            need("pool", (tag + "_v", b))
            put("pool", lambda e: e.tensor_tensor(r[:, d, 0, :], r[:, d, 1, :], half[:, 0:4], ALU.pow), tag + "_r", b)
            need("pool", (tag + "_r", b))
            put("pool", lambda e: e.tensor_tensor(r[:, d, 1, :], m[:, d, :, 0], r[:, d, 0, :], ALU.mult),
                tag + "_m", b)
            need("pool", (tag + "_m", b))
            put("pool", lambda e: e.tensor_scalar(r[:, d, 2, :], r[:, d, 1, :], -1.0, None, ALU.mult), tag + "_m2", b)
            need("pool", (tag + "_m2", b), *war)
            for t in range(4):
                put("pool", lambda e, t=t: e.tensor_scalar(dst[:, t, :], src[:, t, :], r[:, d, 0, t:t + 1],
                                                           r[:, d, 2, t:t + 1], ALU.mult, ALU.add),
                    *((tag + "_n", b) if t == 3 else ()))

        def norm1(k):
            for b in (2 * k, 2 * k + 1):
                for t in range(4):
                    stat(X[:, b % NX, :, :], t, ("x", b), b, stats, mv, "ln")
                    if t % 2:
                        yield
                norm(X[:, b % NX, :, :], ("x", b), b, mv, rs, xn[:, b % 2, :, :], "ln", [("xnT", 2 * (b - 2) + 1)])
                yield

        need("pool", ("cp", chain[0] - 1))
        need("dve", ("cp", chain[0] - 1))
        for _ in norm1(0):
            pass
        mags = [float(np.sqrt(np.float32(1.0 / f) + np.float32(1e-10))) for f in (1, 1, 2, 6, 24)]
        rff = float(np.sqrt(2.0 / (2 * R)) * np.sqrt(np.exp(-0.5)))
        for m in range(5):
            pool(lambda e, m=m: e.memset(wcs[64 * (m % 2):64 * (m % 2) + 64, m // 2:m // 2 + 1], mags[m] * rff))
        need("pool", ("w", 0))
        t8 = lambda i: tmp8[:, i:i + 1]
        pool(lambda e: e.tensor_scalar(t8(0), ltb, -1.0, None, ALU.mult))
        pool(lambda e: e.tensor_tensor(t8(1), ltb, t8(0), ALU.subtract))
        pool(lambda e: e.tensor_scalar(t8(0), ltb, 0.0, None, ALU.max))
        pool(lambda e: e.tensor_scalar(t8(1), t8(0), -2.0, None, ALU.mult))
        pool(lambda e: e.tensor_tensor(t8(1), ltb, t8(1), ALU.add))
        pool(lambda e: e.memset(t8(2), 2.718281828459045))
        pool(lambda e: e.tensor_tensor(t8(3), t8(2), t8(1), ALU.pow))
        pool(lambda e: e.tensor_scalar(t8(3), t8(3), 1.0, None, ALU.add))
        need("act", ("cp", chain[0] - 1))
        put("act", lambda e: e.activation(t8(4), t8(3), ACT.Ln), "ln", 0)
        need("pool", ("ln", 0))
        pool(lambda e: e.tensor_scalar(t8(5), t8(4), -1.0, None, ALU.mult))
        pool(lambda e: e.tensor_tensor(t8(5), t8(2), t8(5), ALU.pow))
        pool(lambda e: e.tensor_tensor(t8(5), t8(5), t8(3), ALU.mult))
        pool(lambda e: e.tensor_scalar(t8(5), t8(5), 1.0, None, ALU.subtract))
        pool(lambda e: e.tensor_tensor(t8(4), t8(4), t8(5), ALU.add))
        pool(lambda e: e.tensor_tensor(t8(4), t8(4), t8(0), ALU.add))
        pool(lambda e: e.tensor_scalar(t8(4), t8(4), 0.1, None, ALU.add))
        pool(lambda e: e.tensor_copy(bcA, bvc.unsqueeze(2).broadcast_to([128, 2, 128])))
        pool(lambda e: e.tensor_copy(bcS, bshc.broadcast_to([64, 128])))
        setup_pool = ("cp", chain[0] - 1)

        dch = [0]

        def dve(fn):
            if dch[0]:
                need("dve", ("cd", dch[0] - 1))
            put("dve", fn, "cd", dch[0])
            dch[0] += 1

        need("dve", setup_pool, ("w", 0))
        dve(lambda e: e.memset(W1[:, :, 353:354], 0.0))
        dve(lambda e: e.memset(biasM[:, 353:354], 0.0))
        dve(lambda e: e.reciprocal(t8(8), t8(4)))
        dve(lambda e: e.tensor_scalar(U[:, :], U[:, :], tmp8[:, 8:9], None, ALU.mult))
        for c in range(2):
            dve(lambda e, c=c: e.tensor_scalar(wc[:, c, :], wc[:, c, :], wcs[:, c:c + 1], None, ALU.mult))
        dve(lambda e: e.tensor_scalar(wc[0:64, 2, :], wc[0:64, 2, :], wcs[0:64, 2:3], None, ALU.mult))
        setup_dve = ("cd", dch[0] - 1)
        dve(lambda e: e.tensor_scalar(tg[:, 0, 0, 0:R], rbB, 1.0 / TWO_PI, MAGIC, ALU.mult, ALU.add))
        dve(lambda e: e.tensor_scalar(tg[:, 0, 0, 0:R], tg[:, 0, 0, 0:R], MAGIC, None, ALU.subtract))
        dve(lambda e: e.scalar_tensor_tensor(tg[:, 0, 1, 0:R], tg[:, 0, 0, 0:R], -PI_HI, rbB, ALU.mult, ALU.add))
        dve(lambda e: e.scalar_tensor_tensor(biasC[:, 1, :], tg[:, 0, 0, 0:R], -PI_LO, tg[:, 0, 1, 0:R],
                                             ALU.mult, ALU.add))
        dve(lambda e: e.tensor_scalar(biasC[:, 0, :], biasC[:, 1, :], TWO_PI / 4, None, ALU.add))

        def setup_mm(w, steps, evac, extra=None):
            i, p = G.take()
            for s, (l, r) in enumerate(steps):
                last = s == len(steps) - 1
                m, n = l.shape[-1], r.shape[-1]
                fn = lambda e, p=p, l=l, r=r, s=s, last=last, m=m, n=n: e.matmul(
                    p[0:m, 0:n], l, r, start=s == 0, stop=last)
                if last:
                    put("pe", fn, "sm", q.counts.get("sm", 0))
                else:
                    put("pe", fn)
            need("dve", ("sm", q.counts["sm"] - 1))
            dve(lambda e, p=p: evac(e, p))
            G.freed[i] = ("cd", dch[0] - 1)

        need("pe", setup_pool, setup_dve, ("w", 0))
        for c in range(2):
            cs = slice(c * 128, c * 128 + 128)
            setup_mm(D, [(wv_n[:, k, cs], woT[:, k, :]) for k in range(2)],
                     lambda e, p, c=c: e.tensor_copy(W1[:, c, 0:256], p[:, 0:256]))
            setup_mm(R, [(wsh[:, cs], omT)], lambda e, p, c=c: e.tensor_copy(W1[:, c, 321:353], p[:, 0:R]))
        setup_mm(D, [(bcA[:, k, :], woT[:, k, :]) for k in range(2)] + [(ones[0:1, :], boutr)],
                 lambda e, p: e.tensor_copy(biasM[:, 0:256], p[:, 0:256]))
        setup_mm(R, [(bcS, omT)], lambda e, p: e.tensor_copy(biasM[:, 321:353], p[:, 0:R]))
        setup_mm(65, [(ones[0:1, :], brow[:, 0:65])], lambda e, p: e.tensor_copy(biasM[:, 256:321], p[:, 0:65]))
        dve(lambda e: e.tensor_copy(W1h[:, :, :], W1))
        dve(lambda e: e.tensor_tensor(W1l[:, :, :], W1, W1h[:, :, :].bitcast(FP), ALU.subtract))
        ready = ("cd", dch[0] - 1)
        for eng in ("pe", "act", "pool"):
            need(eng, ready)

        def slot_setup():
            need("pool", ("wf", 0))
            pool(lambda e: e.tensor_scalar(t8(6), taub, -1.0, None, ALU.mult))
            pool(lambda e: e.tensor_tensor(t8(6), taub, t8(6), ALU.subtract))
            pool(lambda e: e.tensor_scalar(t8(7), taub, 0.0, None, ALU.max))
            pool(lambda e: e.tensor_scalar(t8(7), t8(7), 2.0, None, ALU.mult))
            pool(lambda e: e.tensor_tensor(t8(7), t8(7), taub, ALU.subtract))
            pool(lambda e: e.tensor_scalar(t8(7), t8(7), 0.1, None, ALU.add))

            pool(lambda e: e.tensor_tensor(S0[:, :, :], S0[:, :, :],
                                           sscale.unsqueeze(1).broadcast_to([128, 2, S]), ALU.mult))
            pool(lambda e: e.tensor_copy(bcB, fbvc.unsqueeze(2).broadcast_to([128, 2, 128])))
            pool_done = ("cp", chain[0] - 1)
            need("dve", pool_done, ("wf", 0))
            dve(lambda e: e.reciprocal(t8(9), t8(7)))
            dve(lambda e: e.tensor_scalar(w2[:, :], w2[:, :], t8(9), None, ALU.mult))
            dve(lambda e: e.tensor_scalar(b2[:, :], b2raw, t8(9), None, ALU.mult))
            dve(lambda e: e.tensor_reduce(mslot, S0[:, :, :], AX.X, ALU.add))
            dve(lambda e: e.tensor_scalar(mslot, mslot, 1.0 / S, None, ALU.mult))
            dve(lambda e: e.tensor_tensor(bhh[:, 0:4], bhh[:, 0:4], bihn[:, 0:4], ALU.add))
            yield
            need("pe", pool_done, ("cd", dch[0] - 1), ("wf", 0))
            for c in range(2):
                cs = slice(c * 128, c * 128 + 128)
                setup_mm(D, [(fwv[:, k, cs], fwoT[:, k, :]) for k in range(2)],
                         lambda e, p, c=c: e.tensor_copy(Wvo[:, c, :], p[:, 0:256]))
                yield
            setup_mm(D, [(bcB[:, k, :], fwoT[:, k, :]) for k in range(2)] + [(ones[0:1, :], fbor)],
                     lambda e, p: e.tensor_copy(bSV[:, :], p[:, 0:256]))
            yield
            setup_mm(1, [(w1b[:, k, :], mslot[:, k:k + 1]) for k in range(2)],
                     lambda e, p: e.tensor_tensor(b1[:, :], b1[:, :], p[:, 0:1], ALU.add))
            yield
            for j in range(6):
                setup_mm(S, [(whh[:, k, j * 128:j * 128 + 128], S0[:, k, :]) for k in range(2)],
                         lambda e, p, j=j: e.tensor_scalar(GH[:, j, :], p[:, 0:S], bhh[:, j:j + 1], None, ALU.add))
                if j % 2:
                    yield
            dve(lambda e: e.tensor_scalar(HN[:, :, :], GH[:, 4:6, :], 0.5, None, ALU.mult))
            for eng in ("pe", "act", "pool"):
                need(eng, ("cd", dch[0] - 1))
            yield

        def transposed(srcs, p_src, width, evac_eng, evac, name, n):
            i, p = T.take()
            need("pe", *p_src)
            for j, s in enumerate(srcs):
                m = s.shape[-1]
                fn = lambda e, j=j, s=s, m=m, p=p: e.transpose(p[0:m, j * 128:j * 128 + 128], s, ident[:, :])
                put("pe", fn, *((name + "_t", n) if j == len(srcs) - 1 else ()))
            need(evac_eng, (name + "_t", n))
            put(evac_eng, lambda e, p=p: evac(e, p), name, n)
            T.freed[i] = (name, n)
            return i, p

        def norm2(b):
            norm(x1[:, b % NY, :, :], ("x1", b), b, mv2, rs2, xm[:, b % 4, :, :], "lm",
                 [("xmT", 2 * (b - 4) + 1), ("gi_mm", b - 4)])

        def front(k):
            bs = (2 * k, 2 * k + 1)
            for b in bs:
                d = b % 2
                for c in range(2):
                    need("act", ("vs_mm", 4 * (b - 2) + 3))
                    i, p = transposed([xn[:, d, t, c * 128:c * 128 + 128] for t in range(4)], [("ln_n", b)], 512,
                                      "act", lambda e, p, c=c, d=d: e.activation(xh[:, d, c, :], p[:, :], ACT.Copy),
                                      "xnT", 2 * b + c)
                    need("dve", ("xnT", 2 * b + c), ("vs_mm", 4 * (b - 2) + 3))
                    put("dve", lambda e, c=c, d=d, p=p: e.tensor_tensor(
                        xl[:, d, c, :], p[:, :], xh[:, d, c, :].bitcast(FP), ALU.subtract), "xl", 2 * b + c)
                    T.freed[i] = ("xl", 2 * b + c)
                yield
            for b in bs:
                d = b % 2
                for t in range(4):
                    i, p = G.take()
                    need("pe", ("xnT", 2 * b + 1), ("xl", 2 * b + 1))
                    parts = [(x, w, c) for c in range(2) for x, w in ((xh, W1h), (xh, W1l), (xl, W1h))]
                    for j, (x, w, c) in enumerate(parts):
                        put("pe", lambda e, x=x, w=w, c=c, j=j, t=t, p=p, d=d: e.matmul(
                            p[:, 0:FEATS], x[:, d, c, t * 128:t * 128 + 128], w[:, c, :],
                            start=j == 0, stop=j == 5), *(("vs_mm", 4 * b + t) if j == 5 else ()))
                    need("dve", ("vs_mm", 4 * b + t), ("av", 4 * (b - 4) + 3), ("trig", b // 2 - 2), ("q2", b // 2 - 2))
                    put("dve", lambda e, t=t, p=p, b=b: e.tensor_tensor(VS[:, b % 4, t, :], p[:, 0:FEATS],
                                                                       biasM[:, :], ALU.add), "vs", 4 * b + t)
                    G.freed[i] = ("vs", 4 * b + t)
                    if t == 1:
                        yield
                yield
            v0 = (2 * k) % 4
            VP = VS[:, v0:v0 + 2, :, :]
            need("act", ("vs", 4 * bs[1] + 3), ("tp", bs[1] - 2))
            put("act", lambda e: e.activation(qq[:, :, :, 0:1], VP[:, :, :, 320:321], ACT.Tanh), "q1", k)
            for b in bs:
                d = b % 2
                need("dve", ("vs", 4 * b + 3), ("sin", k - 1))
                put("dve", lambda e, b=b, d=d: e.tensor_tensor(tg[:, d, :, :], VS[:, b % 4, :, 256:320],
                                                              VS[:, b % 4, :, 256:320], ALU.mult), "sq", b)
                need("dve", ("sq", b))
                put("dve", lambda e, d=d: e.tensor_reduce(n2[:, d, 0, :], tg[:, d, :, :], AX.X, ALU.add), "n2", b)
            need("pool", ("n2", bs[1]))
            put("pool", lambda e: e.tensor_scalar(n2[:, :, 1, :], n2[:, :, 0, :], 1e-24, None, ALU.max), "n2m", k)
            need("pool", ("n2m", k))
            put("pool", lambda e: e.tensor_tensor(n2[:, :, 0, :], n2[:, :, 1, :],
                                                  half[:, :].rearrange("p (a b) -> p a b", a=2), ALU.pow), "rn", k)
            need("pool", ("q1", k))
            put("pool", lambda e: e.tensor_tensor(qq[:, :, :, 1:2], qq[:, :, :, 0:1], qq[:, :, :, 0:1], ALU.mult),
                "q2", k)
            need("pool", ("q2", k))
            put("pool", lambda e: e.tensor_tensor(qq[:, :, :, 2:4], qq[:, :, :, 0:2],
                                                  qq[:, :, :, 1:2].broadcast_to([128, 2, 4, 2]), ALU.mult), "q4", k)
            yield
            for b in bs:
                d = b % 2
                need("dve", ("rn", k))
                put("dve", lambda e, b=b, d=d: e.tensor_tensor(
                    tg2[:, d, :, 0:R], VS[:, b % 4, :, 321:353],
                    n2[:, d, 0, :].unsqueeze(2).broadcast_to([128, 4, R]), ALU.mult), "p1", b)
                need("dve", ("p1", b))
                put("dve", lambda e, d=d: e.tensor_tensor(
                    tg[:, d, :, :].rearrange("p t (a r) -> p t a r", a=2),
                    tg2[:, d, :, 0:R].unsqueeze(2).broadcast_to([128, 4, 2, R]),
                    biasC[:, :, :].unsqueeze(1).broadcast_to([128, 4, 2, R]), ALU.add), "p2", b)
            f = lambda z: z[:, :, :, :].rearrange("p d t r -> p (d t r)")
            steps = [
                lambda e: e.tensor_scalar(f(tg2), f(tg), 1.0 / TWO_PI, MAGIC, ALU.mult, ALU.add),
                lambda e: e.tensor_scalar(f(tg2), f(tg2), MAGIC, None, ALU.subtract),
                lambda e: e.scalar_tensor_tensor(f(tg), f(tg2), -PI_HI, f(tg), ALU.mult, ALU.add),
                lambda e: e.scalar_tensor_tensor(f(tg), f(tg2), -PI_LO, f(tg), ALU.mult, ALU.add),
                lambda e: e.tensor_scalar(f(tg), f(tg), PI_CLAMP, -PI_CLAMP, ALU.min, ALU.max),
            ]
            need("dve", ("p2", bs[1]))
            for j, s in enumerate(steps):
                put("dve", s, *(("p3", 5 * k + j) if j < 4 else ("trig", k)))
                if j < 4:
                    need("dve", ("p3", 5 * k + j))
            yield
            yield
            need("act", ("trig", k), ("tp", bs[1] - 2), ("tpT_t", 3 * (bs[1] - 2) + 2))
            put("act", lambda e: e.activation(tp[:, :, :, 0, :], tg[:, :, :, :], ACT.Sin), "sin", k)
            for b in bs:
                d = b % 2
                need("pool", ("sin", k), ("q4", k), ("tpT_t", 3 * (b - 2) + 2))
                put("pool", lambda e, d=d: e.tensor_tensor(
                    tp[:, d, :, 1:5, :], tp[:, d, :, 0:1, :].broadcast_to([128, 4, 4, 64]),
                    qq[:, d, :, :].unsqueeze(3).broadcast_to([128, 4, 4, 64]), ALU.mult), "tp", b)
                yield

        def combine(k):
            bs = (2 * k, 2 * k + 1)
            for b in bs:
                d = b % 2
                tv = tp[:, d, :, :, :].rearrange("p t m r -> p t (m r)")
                for j in range(3):
                    w = 128 if j < 2 else 64
                    need("act", ("phi", k - 1), ("h_mm", b - 4))
                    transposed([tv[:, t, j * 128:j * 128 + w] for t in range(4)], [("tp", b)], 512, "act",
                               lambda e, p, j=j, w=w, d=d: e.activation(tpT(d, j)[0:w, :], p[0:w, :], ACT.Copy),
                               "tpT", 3 * b + j)
                    if j == 1:
                        yield
                yield
            i, p = G.take()
            for j in range(3):
                w = 128 if j < 2 else 64
                for b in bs:
                    d = b % 2
                    need("pe", ("tpT", 3 * b + j))
                    put("pe", lambda e, j=j, w=w, p=p, d=d: e.matmul(
                        p[64 * d:64 * d + C, :], wc[0:w, j, :], tpT(d, j)[0:w, :], start=j == 0, stop=j == 2),
                        *(("phi", k) if j == 2 and b == bs[1] else ()))
            need("dve", ("phi", k), ("lg_mm", 8 * (k - 2) + 7))
            put("dve", lambda e, p=p: e.tensor_tensor(QT[:, k % 2, :], p[:, :], U[:, :], ALU.mult), "QT", k)
            put("dve", lambda e, p=p: e.tensor_tensor(KT[:, k % 2, :], p[:, :], Wk[:, :], ALU.mult), "KT", k)
            G.freed[i] = ("KT", k)
            yield

        def attn(k):
            banks_of = {}
            rows = [(b, i) for b in (2 * k, 2 * k + 1) for i in range(4)]

            def logits(b, i):
                r = 4 * b + i
                w = (i + 1) * 128
                bi, p = L.take()
                need("pe", ("KT", k))
                h = slice(64 * (b % 2), 64 * (b % 2) + 64)
                put("pe", lambda e: e.matmul(p[:, 0:w], QT[h, k % 2, i * 128:w], KT[h, k % 2, 0:w],
                                             start=True, stop=False, skip_group_check=True))
                put("pe", lambda e: e.matmul(p[:, i * 128:w], identb[:, :], maskb[:, :], start=False, stop=True,
                                             skip_group_check=True), "lg_mm", r)
                need("dve", ("lg_mm", r), ("E", r - 8))
                put("dve", lambda e: e.tensor_reduce(nmax[:, r % 8:r % 8 + 1], p[:, 0:w], AX.X, ALU.max,
                                                     negate=True), "nmax", r)
                banks_of[r] = (bi, p)

            def expo(b, i):
                r = 4 * b + i
                w = (i + 1) * 128
                bi, p = banks_of[r]
                need("act", ("nmax", r), ("ET_t", r - 3), ("av", r - 8))
                put("act", lambda e: e.activation(E[:, r % 3, 0:w], p[:, 0:w], ACT.Exp,
                                                  bias=nmax[:, r % 8:r % 8 + 1],
                                                  accum_out=rsum[:, r % 8:r % 8 + 1]), "E", r)
                L.freed[bi] = ("E", r)

            def probs(b, i):
                r = 4 * b + i
                w = (i + 1) * 128
                need("act", ("av_mm", r - 2))
                transposed([E[:, r % 3, j * 128:j * 128 + 128] for j in range(i + 1)], [("E", r)], w, "act",
                           lambda e, p: e.activation(ET[:, r % 2, 0:w], p[:, 0:w], ACT.Copy), "ET", r)

            def values(b, i):
                r = 4 * b + i
                bi, p = O.take()
                need("pe", ("ET", r), ("vs", 4 * b + 3))
                for j in range(i + 1):
                    put("pe", lambda e, j=j: e.matmul(p[:, 0:D], ET[:, r % 2, j * 128:j * 128 + 128],
                                                      VS[:, b % 4, j, 0:256], start=j == 0, stop=j == i),
                        *(("av_mm", r) if j == i else ()))
                need("dve", ("E", r))
                put("dve", lambda e: e.reciprocal(rinv[:, r % 8:r % 8 + 1], rsum[:, r % 8:r % 8 + 1]), "rinv", r)
                need("dve", ("av_mm", r), ("rinv", r), ("st", b - NY))
                put("dve", lambda e: e.scalar_tensor_tensor(
                    x1[:, b % NY, i, :], p[:, 0:D], rinv[:, r % 8:r % 8 + 1], X[:, b % NX, i, :],
                    ALU.mult, ALU.add), "av", r)
                O.freed[bi] = ("av", r)
                if i == 3:
                    q.at[("x1", b)] = q.at[("av", r)]

            for n in range(len(rows) + 4):
                if 1 <= n <= len(rows):
                    expo(*rows[n - 1])
                if n < len(rows):
                    logits(*rows[n])
                if 2 <= n <= len(rows) + 1:
                    probs(*rows[n - 2])
                if 3 <= n <= len(rows) + 2:
                    values(*rows[n - 3])
                if n >= 4:
                    b, i = rows[n - 4]
                    stat(x1[:, b % NY, :, :], i, ("av", 4 * b + i), b, stats2, mv2, "lm")
                    if i == 3:
                        norm2(b)
                yield

        def back(k):
            bs = (2 * k, 2 * k + 1)
            for b in bs:
                d = b % 2
                for c in range(2):
                    need("act", ("h_mm", b - 2), ("phi", min(k + 1, B // 2 - 1)))
                    transposed([xm[:, b % 4, t, c * 128:c * 128 + 128] for t in range(4)], [("lm_n", b)], 512, "act",
                               lambda e, p, c=c, d=d: e.activation(xmT[:, d, c, :], p[:, :], ACT.Copy),
                               "xmT", 2 * b + c)
                yield
            held = []
            for b in bs:
                d = b % 2
                i, p = G.take()
                held.append((i, p))
                need("pe", ("xmT", 2 * b + 1))
                for c in range(2):
                    put("pe", lambda e, c=c, p=p, d=d: e.matmul(p[:, :], w1a[:, c, :], xmT[:, d, c, :],
                                                              start=c == 0, stop=c == 1),
                        *(("h_mm", b) if c else ()))
            for b, (i, p) in zip(bs, held):
                d = b % 2
                need("act", ("h_mm", b), ("rt_mm", b - 2))
                put("act", lambda e, p=p, d=d: e.activation(hT[:, d, :], p[:, :], ACT.Gelu, bias=b1[:, 0:1]), "h", b)
                G.freed[i] = ("h", b)
            yield
            for b in bs:
                d = b % 2
                i, p = G.take()
                need("pe", ("h", b))
                for t in range(4):
                    put("pe", lambda e, t=t, p=p, d=d: e.matmul(p[:, t * S:t * S + S], hT[:, d, t * 128:t * 128 + 128],
                                                              w2[:, :], start=True, stop=True, skip_group_check=True),
                        *(("rt_mm", b) if t == 3 else ()))
                need("dve", ("rt_mm", b), ("al", b - 2))
                put("dve", lambda e, p=p, d=d: e.tensor_tensor(
                    lg[:, d, 0, :, :], p[:, 0:4 * S].rearrange("p (t s) -> p t s", t=4),
                    b2[:, :].unsqueeze(1).broadcast_to([128, 4, S]), ALU.add), "lg", b)
                G.freed[i] = ("lg", b)
                need("dve", ("lg", b))
                for t in range(4):
                    put("dve", lambda e, t=t, d=d: e.max(m8[:, d, t, :], lg[:, d, 0, t, :]), "m8", 4 * b + t)
                for t in range(4):
                    need("dve", ("m8", 4 * b + t))
                    put("dve", lambda e, t=t, d=d: e.match_replace(lg[:, d, 1, t, :], m8[:, d, t, :],
                                                                  lg[:, d, 0, t, :], -3e38), "mr", 4 * b + t)
                need("pool", ("mr", 4 * b + 3))
                for z in range(2):
                    put("pool", lambda e, d=d, z=z: e.tensor_tensor(
                        lg[:, d, z, :, :], lg[:, d, z, :, :],
                        m8[:, d, :, 0:1].broadcast_to([128, 4, S]), ALU.subtract), *(("dm", b) if z else ()))
                yield
            for b in bs:
                d = b % 2
                need("act", ("dm", b))
                put("act", lambda e, d=d: e.activation(lg[:, d, :, :, :], lg[:, d, :, :, :], ACT.Exp), "ex", b)
                need("pool", ("ex", b))
                put("pool", lambda e, d=d: e.tensor_tensor(lg[:, d, 0, :, :], lg[:, d, 0, :, :], lg[:, d, 1, :, :],
                                                          ALU.subtract), "am0", b)
                yield
            for _ in range(PAUSE):
                yield
            for b in bs:
                d = b % 2
                need("dve", ("am0", b))
                put("dve", lambda e, d=d: e.tensor_reduce(asum[:, d, 0, :], lg[:, d, 0, :, :], AX.X, ALU.add),
                    "as0", b)
                need("dve", ("as0", b))
                put("dve", lambda e, d=d: e.reciprocal(asum[:, d, 1, :], asum[:, d, 0, :]), "as1", b)
                need("pool", ("as1", b), ("aT_t", k - 2), ("gi_mm", b - 4))
                put("pool", lambda e, d=d: e.tensor_tensor(
                    AL[:, k % 2, :, d, :], lg[:, d, 0, :, :],
                    asum[:, d, 1, :].unsqueeze(2).broadcast_to([128, 4, S]), ALU.mult), "am", b)
                need("pool", ("am", b), ("gi_mm", b - 2))
                put("pool", lambda e, d=d: e.tensor_tensor(lg[:, d, 1, 0:2, :], AL[:, k % 2, 0:2, d, :],
                                                          AL[:, k % 2, 2:4, d, :], ALU.add), "al0", b)
                need("pool", ("al0", b))
                put("pool", lambda e, d=d: e.tensor_tensor(alt[:, d, :], lg[:, d, 1, 0, :], lg[:, d, 1, 1, :],
                                                          ALU.add), "al", b)
                yield
            for b in bs:
                d = b % 2
                i, p = G.take()
                need("pe", ("am", b), ("al", b), ("lm_n", b))
                for c in range(2):
                    for t in range(4):
                        put("pe", lambda e, c=c, t=t, p=p, d=d, b=b: e.matmul(
                            p[:, c * S:c * S + S], xm[:, b % 4, t, c * 128:c * 128 + 128], AL[:, k % 2, t, d, :],
                            start=t == 0, stop=t == 3))
                put("pe", lambda e, p=p, d=d: e.matmul(p[:, 2 * S:3 * S], ones[:, :], alt[:, d, :],
                                                     start=True, stop=True), "gi_mm", b)
                need("dve", ("gi_mm", b), ("gi", b - 1))
                put("dve", lambda e, p=p: e.tensor_scalar(rw[:, :], p[:, 2 * S:3 * S], 1e-8, None, ALU.add), "rw0", b)
                need("dve", ("rw0", b))
                put("dve", lambda e: e.reciprocal(rw[:, :], rw[:, :]), "rw", b)
                need("dve", ("rw", b), ("gx_mm", k - 2))
                put("dve", lambda e, p=p, d=d: e.tensor_tensor(
                    GI[:, k % 2, :, d, :], p[:, 0:2 * S].rearrange("p (c s) -> p c s", c=2),
                    rw[:, :].unsqueeze(1).broadcast_to([128, 2, S]), ALU.mult), "gi", b)
                G.freed[i] = ("gi", b)
                yield

        def slots(k):
            i1, p1 = G.take()
            need("pe", ("gi", 2 * k + 1))
            gx = lambda j, c: (wih[:, c, j * 128:j * 128 + 128], GI[:, k % 2, c, :, :].rearrange("p b s -> p (b s)"))
            for j in range(4):
                for c in range(2):
                    put("pe", lambda e, j=j, c=c: e.matmul(p1[:, j * 128:j * 128 + 128], *gx(j, c),
                                                           start=c == 0, stop=c == 1),
                        *(("rz_mm", k) if j == 3 and c else ()))
            need("dve", ("rz_mm", k))
            put("dve", lambda e: e.tensor_tensor(
                grz[:, :, :, :], p1[:, :].rearrange("p (j b s) -> p j b s", j=4, b=2),
                GH[:, 0:4, :].unsqueeze(2).broadcast_to([128, 4, 2, S]), ALU.add), "grz", k)
            G.freed[i1] = ("grz", k)
            yield
            need("act", ("grz", k))
            fl = lambda z: z.rearrange("p c b s -> p (c b s)")
            put("act", lambda e: e.activation(fl(grz[:, :, :, :]), fl(grz[:, :, :, :]), ACT.Tanh, scale=0.5), "srz", k)
            yield
            i2, p2 = G.take()
            for j in range(2):
                for c in range(2):
                    put("pe", lambda e, j=j, c=c: e.matmul(p2[:, j * 128:j * 128 + 128], *gx(4 + j, c),
                                                           start=c == 0, stop=c == 1),
                        *(("gx_mm", k) if j and c else ()))
            need("dve", ("srz", k))
            put("dve", lambda e: e.scalar_tensor_tensor(
                gt[:, 0, :, :], grz[:, 0, :, :], 1.0,
                HN[:, 0, :].unsqueeze(1).broadcast_to([128, 2, S]), ALU.add, ALU.mult))
            put("dve", lambda e: e.scalar_tensor_tensor(
                gt[:, 1, :, :], grz[:, 1, :, :], 1.0,
                HN[:, 1, :].unsqueeze(1).broadcast_to([128, 2, S]), ALU.add, ALU.mult), "rhn", k)
            need("dve", ("rhn", k), ("gx_mm", k))
            put("dve", lambda e: e.tensor_tensor(fl(gn[:, :, :, :]), p2[:, 0:256], fl(gt[:, :, :, :]), ALU.add),
                "gn", k)
            G.freed[i2] = ("gn", k)
            need("act", ("gn", k))
            for c in range(2):
                put("act", lambda e, c=c: e.activation(gn[:, c, :, :], gn[:, c, :, :], ACT.Tanh,
                                                       bias=bihn[:, 4 + c:5 + c]), *(("nn", k) if c else ()))
            yield
            need("pool", ("nn", k))
            put("pool", lambda e: e.tensor_tensor(
                gt[:, :, :, :], S0[:, :, :].unsqueeze(2).broadcast_to([128, 2, 2, S]), gn[:, :, :, :],
                ALU.subtract), "hd", k)
            yield
            need("dve", ("hd", k))
            put("dve", lambda e: e.scalar_tensor_tensor(fl(gt[:, :, :, :]), fl(grz[:, 2:4, :, :]), 1.0,
                                                        fl(gt[:, :, :, :]), ALU.add, ALU.mult), "hz", k)
            need("dve", ("hz", k), ("sv_mm", k - 1))
            put("dve", lambda e: e.scalar_tensor_tensor(fl(SN[:, :, :, :]), fl(gt[:, :, :, :]), 0.5,
                                                        fl(gn[:, :, :, :]), ALU.mult, ALU.add), "sn", k)
            need("act", ("of_mm", 4 * (k - 2) + 3))
            transposed([AL[:, k % 2, t, :, :].rearrange("p b s -> p (b s)") for t in range(4)],
                       [("am", 2 * k + 1)], 512, "act",
                       lambda e, p: e.activation(aT[:, k % 2, :], p[:, :], ACT.Copy), "aT", k)
            yield
            i3, p3 = G.take()
            need("pe", ("sn", k))
            for c in range(2):
                put("pe", lambda e, c=c: e.matmul(p3[:, 0:D], SN[:, c, :, :].rearrange("p b s -> p (b s)"),
                                                  Wvo[:, c, :], start=c == 0, stop=c == 1),
                    *(("sv_mm", k) if c else ()))
            need("dve", ("sv_mm", k), ("of_mm", 4 * (k - 2) + 3))
            put("dve", lambda e: e.tensor_tensor(SV[:, k % 2, :], p3[:, 0:D], bSV[:, :], ALU.add), "sv", k)
            G.freed[i3] = ("sv", k)
            yield
            for b in (2 * k, 2 * k + 1):
                h = slice(64 * (b % 2), 64 * (b % 2) + 64)
                for t in (0, 2):
                    bi, p = G.take()
                    need("pe", ("aT", k), ("sv", k))
                    for u in range(2):
                        put("pe", lambda e, t=t + u, u=u, p=p, h=h: e.matmul(
                            p[:, u * D:u * D + D], aT[h, k % 2, t * 128:t * 128 + 128], SV[h, k % 2, :],
                            start=True, stop=True), *(("of_mm", 2 * b + t // 2) if u else ()))
                    need("dve", ("of_mm", 2 * b + t // 2), ("lm_n", b))
                    xv = x1[:, b % NY, t:t + 2, :]
                    put("dve", lambda e, xv=xv, p=p: e.tensor_tensor(
                        xv, p[:, :].rearrange("p (t d) -> p t d", t=2), xv, ALU.add), "fin", 2 * b + t // 2)
                    G.freed[bi] = ("fin", 2 * b + t // 2)
                    if t == 0:
                        yield
                need("sp", ("fin", 2 * b + 1))
                put("sp", lambda e, b=b: e.dma_start(out[b].rearrange("(t p) d -> p t d", p=128), x1[:, b % NY, :, :]),
                    "st", b, sem=f"st{b % NY}", by=16)
                yield

        NP = B // 2
        for it in range(NP + 3):
            work = [(kind, stage(it - lag)) for kind, stage, lag in
                    (("F", front, 0), ("C", combine, 0), ("N", norm1, -1), ("A", attn, 1), ("B", back, 2), ("S", slots, 3))
                    if 0 <= it - lag < NP]
            if it == 0:
                work.append(("W", slot_setup()))
            turns = sorted((at, n) for n, (kind, _) in enumerate(work) for at in PLACES[kind])
            for _, n in turns:
                next(work[n][1])
            for kind, g in work:
                assert next(g, "end") == "end", kind
            for b in (2 * it + 4, 2 * it + 5):
                if b < B:
                    load_x(b)
        need("sp", *[("st", b) for b in range(B)])

        block = ctx.enter_context(nc.Block())

        @block.sync
        def _(e):
            for fn in q.lists["sp"]:
                fn(e)

        @block.gpsimd
        def _(e):
            for fn in q.lists["pool"]:
                fn(e)

        @block.scalar
        def _(e):
            for fn in q.lists["act"]:
                fn(e)

        @block.vector
        def _(e):
            for fn in q.lists["dve"]:
                fn(e)

        @block.tensor
        def _(e):
            for fn in q.lists["pe"]:
                fn(e)


PAUSE = 1
PLACES = dict(
    F=(0.000, 0.000, 0.000, 0.015, 0.064, 0.076, 0.112, 0.225, 0.250, 0.359, 0.375),
    C=(0.571, 0.632, 0.722, 0.775, 0.829),
    N=(0.402, 0.522, 0.548, 0.644, 0.732, 0.772),
    A=(0.017, 0.125, 0.208, 0.249, 0.354, 0.458, 0.542, 0.625, 0.656, 0.792, 0.869, 0.901),
    B=(0.000, 0.154, 0.238, 0.321, 0.466, 0.587, 0.590, 0.645, 0.663, 0.737, 0.959, 0.964),
    S=(0.170, 0.213, 0.255, 0.308, 0.392, 0.471, 0.551, 0.737, 0.761, 0.957),
    W=(0.056, 0.167, 0.278, 0.389, 0.500, 0.611, 0.722, 0.833, 0.944),
)


def kernel(**inputs):
    import concourse.bacc as bacc
    from concourse.bass_utils import run_bass_kernel_spmd

    g = {k: np.asarray(v) for k, v in inputs.items()}
    at, ff = "L0_attn_", "L0_ffn_"
    con = np.ascontiguousarray
    ramp = np.arange(N, dtype=np.float64) - (N - 1) / 2
    arrays = {
        "x": g[at + "x"],
        "b_charge": g[at + "b_charge"],
        "W_shell": g[at + "W_shell"],
        "W_scT": con(np.concatenate([g[at + "W_shell"], g[at + "W_charge"]]).T),
        "b_shell": g[at + "b_shell"],
        "omegaT": con(g[at + "omega"].T),
        "rff_bias": g[at + "rff_bias"],
        "W_combineT": con(g[at + "W_combine"].T),
        "W_v": g[at + "W_v"],
        "b_v": con(g[at + "b_v"].reshape(2, 128).T),
        "W_outT": con(g[at + "W_out"].T),
        "b_out": g[at + "b_out"],
        "log_temp": con(g[at + "log_temp"].reshape(1)),
        "decay": np.stack([np.exp(-0.03 * ramp), np.exp(0.03 * ramp)]).astype(np.float32),
        "slot_initT": con(g[ff + "slot_init"].T),
        "slot_scale": con(g[ff + "slot_scale"].reshape(-1)),
        "w1T": con(g[ff + "w1"].T),
        "b1": g[ff + "b1"],
        "w2T": con(g[ff + "w2"].T),
        "b2": g[ff + "b2"],
        "gru_wihT": con(g[ff + "gru_wih"].T),
        "gru_whhT": con(g[ff + "gru_whh"].T),
        "gru_bih": con(g[ff + "gru_bih"].reshape(6, 128).T),
        "gru_bhh": con(g[ff + "gru_bhh"].reshape(6, 128).T),
        "wv": g[ff + "wv"],
        "bv": con(g[ff + "bv"].reshape(2, 128).T),
        "woT": con(g[ff + "wo"].T),
        "bo": g[ff + "bo"],
        "tau": g[ff + "tau"],
    }
    nc = bacc.Bacc("TRN2", target_bir_lowering=False, num_devices=1)
    aps = {k: nc.dram_tensor("in_" + k, v.shape, mybir.dt.from_np(v.dtype), kind="ExternalInput").ap()
           for k, v in arrays.items()}
    out = nc.dram_tensor("out_x", (B, N, D), FP, kind="ExternalOutput").ap()
    build(nc, aps, out)
    r = run_bass_kernel_spmd(nc, [{"in_" + k: v for k, v in arrays.items()}], core_ids=[0])
    return r.results[0]["out_x"]
```

```python
import numpy as np
import concourse.bass as bass
from concourse import mybir
from contextlib import ExitStack

B, N, D = 32, 512, 256
S, H, R, C = 64, 128, 32, 64
ORDER = 4
FP = mybir.dt.float32
BF = mybir.dt.bfloat16
FR = mybir.dt.float32r
ALU = mybir.AluOpType
ACT = mybir.ActivationFunctionType
AX = mybir.AxisListType
MAGIC = 12582912.0
TWO_PI = 6.283185307179586
PI_HI = 6.28125
PI_LO = TWO_PI - PI_HI
PI_CLAMP = 3.1415925
FEATS = 354


class Queues:

    def __init__(self, nc, ctx):
        self.nc, self.ctx = nc, ctx
        self.lists = {k: [] for k in ("pe", "act", "dve", "pool", "sp")}
        self.sems, self.counts, self.at, self.seen = {}, {}, {}, {}

    def sem(self, name):
        if name not in self.sems:
            self.sems[name] = self.ctx.enter_context(self.nc.semaphore("s_" + name))
            self.counts[name] = 0
        return self.sems[name]

    def need(self, eng, *products):
        for name, n in products:
            if n < 0:
                continue
            sem, value = self.at[(name, n)]
            if self.seen.get((eng, sem), 0) >= value:
                continue
            self.seen[(eng, sem)] = value
            s = self.sems[sem]
            self.lists[eng].append(lambda e, s=s, v=value: e.wait_ge(s, v))

    def put(self, eng, fn, name=None, n=0, sem=None, by=1):
        if name is None:
            self.lists[eng].append(fn)
            return
        sem = sem or name
        s = self.sem(sem)
        self.counts[sem] += by
        self.at[(name, n)] = (sem, self.counts[sem])
        self.lists[eng].append(lambda e: fn(e).then_inc(s, by))


class Banks:

    def __init__(self, q, tensors):
        self.q, self.tensors, self.n = q, tensors, 0
        self.freed = [None] * len(tensors)

    def take(self):
        i = self.n % len(self.tensors)
        self.n += 1
        if self.n > len(self.tensors):
            assert self.freed[i] is not None, "taken again before its reader is queued"
            self.q.need("pe", self.freed[i])
        self.freed[i] = None
        return i, self.tensors[i]


def build(nc, a, out):
    ctx = ExitStack()
    with ctx:
        q = Queues(nc, ctx)
        need, put = q.need, q.put

        def sb(name, shape, dt=FP):
            return ctx.enter_context(nc.sbuf_tensor(name, shape, dt))

        banks = [ctx.enter_context(nc.psum_tensor(f"ps{i}", [128, 512], FP)) for i in range(8)]
        T = Banks(q, [banks[0], banks[1], banks[7]])
        L = Banks(q, banks[2:4])
        G = Banks(q, banks[4:7])

        ident = sb("ident", [128, 128])
        identb = sb("identb", [128, 128], BF)
        maskb = sb("maskb", [128, 128], BF)
        ones = sb("ones", [128, 128])
        W1h = sb("W1h", [128, 2, FEATS], FR)
        W1l = sb("W1l", [128, 2, FEATS], FR)
        biasM = sb("biasM", [128, FEATS])
        biasC = sb("biasC", [128, 2, R])
        wc = sb("wc", [128, 3, C])
        wcs = sb("wcs", [128, 3])
        U = sb("U", [128, N])
        Wk = sb("Wk", [128, N])
        w1a = sb("w1a", [128, 2, H])
        b1 = sb("b1", [128, 1])
        w2 = sb("w2", [128, S])
        b2 = sb("b2", [128, S])
        wih = sb("wih", [128, 2, 3 * D])
        GH = sb("GH", [128, 6, S])
        HN = sb("HN", [128, 2, S])
        bihn = sb("bihn", [128, 6])
        S0 = sb("S0", [128, 2, S])
        Wvo = sb("Wvo", [128, 2, D])
        bSV = sb("bSV", [128, D])
        half = sb("half", [128, 8])

        NX = 10
        X = sb("X", [128, NX, 4, D])
        stats = sb("stats", [128, 2, 4, 6])
        mv = sb("mv", [128, 2, 4, 2])
        rs = sb("rs", [128, 2, 3, 4])
        xn = sb("xn", [128, 2, 4, D])
        xh = sb("xh", [128, 2, 2, N], FR)
        xl = sb("xl", [128, 2, 2, N], FR)
        VS = sb("VS", [128, 4, 4, FEATS])
        tg = sb("tg", [128, 2, 4, 2 * R])
        tg2 = sb("tg2", [128, 2, 4, 2 * R])
        qq = sb("qq", [128, 2, 4, 4])
        n2 = sb("n2", [128, 2, 2, 4])
        tp = sb("tp", [128, 2, 4, 5, 64])
        tpT2 = sb("tpT2", [64, 2, N])
        QS = sb("QS", [128, 2, N], FR)
        KS = sb("KS", [128, 2, N], FR)
        Ql = sb("Ql", [128, N], FR)
        Kl = sb("Kl", [128, N], FR)
        nmax = sb("nmax", [128, 8])
        rsum = sb("rsum", [128, 8])
        rinv = sb("rinv", [128, 8])
        E = sb("E", [128, 3, N])
        ET = sb("ET", [128, 2, N])
        stats2 = sb("stats2", [128, 2, 4, 6])
        mv2 = sb("mv2", [128, 2, 4, 2])
        rs2 = sb("rs2", [128, 2, 3, 4])
        xm = sb("xm", [128, 4, 4, D])
        xmT = sb("xmT", [128, 2, 2, N])
        hT = sb("hT", [128, 2, N])
        lg = sb("lg", [128, 2, 2, 4, S])
        m8 = sb("m8", [128, 2, 4, 8])
        asum = sb("asum", [128, 2, 2, 4])
        AL = sb("AL", [128, 2, 4, 2, S])
        alt = sb("alt", [128, 2, S])
        rw = sb("rw", [128, S])
        GI = sb("GI", [128, 2, 2, 2, S])
        grz = sb("grz", [128, 4, 2, S])
        gn = sb("gn", [128, 2, 2, S])
        gt = sb("gt", [128, 2, 2, S])
        SN = sb("SN", [128, 2, 2, S])
        SVS = sb("SVS", [128, 2, D], FR)
        SVl = sb("SVl", [128, D], FR)
        AS = sb("AS", [128, 2, N], FR)
        aTl = sb("aTl", [128, N], FR)

        def own(d):
            return slice(64 * d, 64 * d + 64)

        def oth(d):
            return own(1 - d)

        def tpT(d, j):
            return xmT[:, d, j, :] if j < 2 else tpT2[:, d, :]

        wv_n = X[:, 4, 0:2, :]
        woT = X[:, 4, 2:4, :]
        fwv = X[:, 5, 0:2, :]
        fwoT = X[:, 5, 2:4, :]
        whh = X[:, 6:8, :, :].rearrange("p a t d -> p (a t d)")[:, 0:2 * 3 * D].rearrange("p (c n) -> p c n", c=2)
        stg = X[:, 8, :, :].rearrange("p t d -> p (t d)")
        bvc = stg[:, 0:2]
        boutr = stg[0:1, 8:8 + D]
        fbvc = stg[:, 2:4]
        fbor = stg[0:1, 264:264 + D]
        wsh = stg[0:64, 520:776]
        omT = stg[0:64, 776:808]
        bshc = stg[0:64, 808:809]
        brow = stg[0:1, 812:812 + 65]
        rbB = stg[:, 880:912]
        mslot = stg[:, 912:914]
        bhh = stg[:, 914:920]
        ltb = stg[:, 920:921]
        taub = stg[:, 921:922]
        tmp8 = stg[:, 922:938]
        stg2 = X[:, 9, :, :].rearrange("p t d -> p (t d)")
        w1b = stg2[:, 0:2 * H].rearrange("p (c n) -> p c n", c=2)
        sscale = stg2[:, 256:320]
        bcA = stg2[:, 320:320 + 256].rearrange("p (c n) -> p c n", c=2)
        bcB = stg2[:, 576:576 + 256].rearrange("p (c n) -> p c n", c=2)
        bcS = stg2[0:64, 832:960]
        b2raw = stg2[:, 960:1024]
        W1 = VS[:, 3, 0:2, :]

        setup_done = []

        def load(dst, src, product="w"):
            eng = "sp" if product == "w" else "act"
            put(eng, lambda e, d=dst, s=src: e.dma_start(d, s), product, 0, by=16)

        def loada(dst, src):
            load(dst, src, "wa")

        def loadb(dst, src):
            load(dst, src, "wb")

        def loadf(dst, src):
            load(dst, src, "wf")

        def chunks(ap, c=2):
            return ap.rearrange("(c p) n -> p c n", c=c)

        def load_x(b):
            need("sp", ("st", b - NX))
            if 4 <= b < NX:
                need("sp", *setup_done)
            put("sp", lambda e, b=b: e.dma_start(X[:, b % NX, :, :], a["x"][b].rearrange("(t p) d -> p t d", p=128)),
                "x", b, sem=f"x{b % NX}", by=16)

        load_x(0)
        load_x(1)
        loada(wv_n, chunks(a["W_v"]))
        loada(woT, chunks(a["W_outT"]))
        loada(wsh, a["W_shell"])
        loada(omT, a["omegaT"])
        loadb(W1[:, :, 256:321], chunks(a["W_scT"]))
        loadb(bshc, a["b_shell"].rearrange("(p a) -> p a", a=1))
        loadb(bvc, a["b_v"])
        loadb(boutr, a["b_out"].rearrange("(a n) -> a n", a=1))
        loadb(brow[:, 0:64], a["b_shell"].rearrange("(a n) -> a n", a=1))
        loadb(brow[:, 64:65], a["b_charge"].rearrange("(a n) -> a n", a=1))
        load(ltb, a["log_temp"].partition_broadcast(128))
        load(rbB, a["rff_bias"].partition_broadcast(128))
        load(wc[:, 0:2, :], a["W_combineT"][0:256, :].rearrange("(c p) n -> p c n", c=2))
        load(wc[0:64, 2, :], a["W_combineT"][256:320, :])
        load(U[:, :], a["decay"][0, :].partition_broadcast(128))
        load(Wk[:, :], a["decay"][1, :].partition_broadcast(128))
        loadf(fwv, chunks(a["wv"]))
        loadf(fwoT, chunks(a["woT"]))
        loadf(fbvc, a["bv"])
        loadf(fbor, a["bo"].rearrange("(a n) -> a n", a=1))
        loadf(whh, chunks(a["gru_whhT"]))
        loadf(wih[:, :, :], chunks(a["gru_wihT"]))
        loadf(w1a[:, :, :], chunks(a["w1T"][0:256, :]))
        loadf(w1b, chunks(a["w1T"][256:512, :]))
        loadf(b1[:, :], a["b1"].rearrange("(p a) -> p a", a=1))
        loadf(w2[:, :], a["w2T"])
        loadf(b2raw, a["b2"].partition_broadcast(128))
        loadf(bihn[:, :], a["gru_bih"])
        loadf(bhh, a["gru_bhh"])
        loadf(S0[:, :, :], chunks(a["slot_initT"]))
        loadf(sscale, a["slot_scale"].partition_broadcast(128))
        loadf(taub, a["tau"].partition_broadcast(128))
        load_x(2)
        load_x(3)

        chain = [0]

        def pool(fn, last=None):
            if chain[0]:
                need("pool", ("cp", chain[0] - 1))
            put("pool", fn, "cp", chain[0])
            chain[0] += 1

        pool(lambda e: e.memset(ident[:, :], 0.0))
        pool(lambda e: e.affine_select(out=ident[:, :], in_=ident[:, :], compare_op=ALU.not_equal, fill=1.0,
                                       base=0, pattern=[[-1, 128]], channel_multiplier=1))
        pool(lambda e: e.memset(identb[:, :], 0.0))
        pool(lambda e: e.affine_select(out=identb[:, :], in_=identb[:, :], compare_op=ALU.not_equal, fill=1.0,
                                       base=0, pattern=[[-1, 128]], channel_multiplier=1))
        pool(lambda e: e.memset(maskb[:, :], 0.0))
        pool(lambda e: e.affine_select(out=maskb[:, :], in_=maskb[:, :], compare_op=ALU.is_ge, fill=-1e30,
                                       base=0, pattern=[[-1, 128]], channel_multiplier=1))
        pool(lambda e: e.memset(ones[:, :], 1.0))
        pool(lambda e: e.memset(half[:, :], -0.5))
        def stat(src, t, src_p, b, st, tag):
            d = b % 2
            need("dve", src_p, (tag + "_n", b - 2))
            put("dve", lambda e: e.bn_stats(st[:, d, t, :], src[:, t, :]), tag + "_s", 4 * b + t)

        def aggr(t, b, st, m, tag):
            d = b % 2
            need("dve", (tag + "_s", 4 * b + t))
            put("dve", lambda e: e.bn_aggr(m[:, d, t, :], st[:, d, t, :]), tag + "_a", 4 * b + t)

        def norm(src, src_p, b, m, r, dst, tag, war):
            d = b % 2
            need("pool", (tag + "_a", 4 * b + 3), src_p)
            put("pool", lambda e: e.tensor_scalar(r[:, d, 1, :], m[:, d, :, 1], 1e-5, None, ALU.add), tag + "_v", b)
            need("pool", (tag + "_v", b))
            put("pool", lambda e: e.tensor_tensor(r[:, d, 0, :], r[:, d, 1, :], half[:, 0:4], ALU.pow), tag + "_r", b)
            need("pool", (tag + "_r", b))
            put("pool", lambda e: e.tensor_tensor(r[:, d, 1, :], m[:, d, :, 0], r[:, d, 0, :], ALU.mult),
                tag + "_m", b)
            need("pool", (tag + "_m", b))
            put("pool", lambda e: e.tensor_scalar(r[:, d, 2, :], r[:, d, 1, :], -1.0, None, ALU.mult), tag + "_m2", b)
            need("pool", (tag + "_m2", b), *war)
            for t in range(4):
                put("pool", lambda e, t=t: e.tensor_scalar(dst[:, t, :], src[:, t, :], r[:, d, 0, t:t + 1],
                                                           r[:, d, 2, t:t + 1], ALU.mult, ALU.add),
                    *((tag + "_n", b) if t == 3 else ()))

        def norm1(k):
            for b in (2 * k, 2 * k + 1):
                for t in range(4):
                    stat(X[:, b % NX, :, :], t, ("x", b), b, stats, "ln")
                    if t % 2:
                        aggr(t - 1, b, stats, mv, "ln")
                        aggr(t, b, stats, mv, "ln")
                        yield
                norm(X[:, b % NX, :, :], ("x", b), b, mv, rs, xn[:, b % 2, :, :], "ln", [("xnT", 2 * (b - 2) + 1)])
                yield

        consts = ("cp", chain[0] - 1)
        for eng in ("pe", "dve", "pool"):
            need(eng, consts)
        for _ in norm1(0):
            pass
        need("pool", ("wb", 0))
        pool(lambda e: e.tensor_copy(bcA, bvc.unsqueeze(2).broadcast_to([128, 2, 128])))
        pool(lambda e: e.tensor_copy(bcS, bshc.broadcast_to([64, 128])))
        columns = ("cp", chain[0] - 1)

        dch = [0]

        def dve(fn):
            if dch[0]:
                need("dve", ("cd", dch[0] - 1))
            put("dve", fn, "cd", dch[0])
            dch[0] += 1

        def setup_mm(steps, evac):
            i, p = G.take()
            for s, (l, r) in enumerate(steps):
                last = s == len(steps) - 1
                m, n = l.shape[-1], r.shape[-1]
                fn = lambda e, p=p, l=l, r=r, s=s, last=last, m=m, n=n: e.matmul(
                    p[0:m, 0:n], l, r, start=s == 0, stop=last)
                if last:
                    put("pe", fn, "sm", q.counts.get("sm", 0))
                else:
                    put("pe", fn)
            need("dve", ("sm", q.counts["sm"] - 1))
            dve(lambda e, p=p: evac(e, p))
            G.freed[i] = ("cd", dch[0] - 1)

        dve(lambda e: e.memset(W1[:, :, 353:354], 0.0))
        dve(lambda e: e.memset(biasM[:, 353:354], 0.0))
        need("pe", ("wa", 0))
        need("dve", ("wa", 0))
        for c in range(2):
            cs = slice(c * 128, c * 128 + 128)
            setup_mm([(wv_n[:, k, cs], woT[:, k, :]) for k in range(2)],
                     lambda e, p, c=c: e.tensor_copy(W1[:, c, 0:256], p[:, 0:256]))
            setup_mm([(wsh[:, cs], omT)], lambda e, p, c=c: e.tensor_copy(W1[:, c, 321:353], p[:, 0:R]))
        need("dve", ("wb", 0))
        dve(lambda e: e.tensor_copy(W1h[:, :, :], W1))
        dve(lambda e: e.tensor_tensor(W1l[:, :, :], W1, W1h[:, :, :].bitcast(FP), ALU.subtract))
        need("pe", ("wb", 0))
        setup_mm([(ones[0:1, :], brow[:, 0:65])], lambda e, p: e.tensor_copy(biasM[:, 256:321], p[:, 0:65]))
        need("pe", columns)
        setup_mm([(bcA[:, k, :], woT[:, k, :]) for k in range(2)] + [(ones[0:1, :], boutr)],
                 lambda e, p: e.tensor_copy(biasM[:, 0:256], p[:, 0:256]))
        setup_mm([(bcS, omT)], lambda e, p: e.tensor_copy(biasM[:, 321:353], p[:, 0:R]))
        projection = ("cd", dch[0] - 1)

        mags = [float(np.sqrt(np.float32(1.0 / f) + np.float32(1e-10))) for f in (1, 1, 2, 6, 24)]
        rff = float(np.sqrt(2.0 / (2 * R)) * np.sqrt(np.exp(-0.5)))

        t8 = lambda i: tmp8[:, i:i + 1]

        def attn_setup():
            for m in range(5):
                pool(lambda e, m=m: e.memset(wcs[64 * (m % 2):64 * (m % 2) + 64, m // 2:m // 2 + 1], mags[m] * rff))
            need("pool", ("w", 0))
            pool(lambda e: e.tensor_scalar(t8(0), ltb, -1.0, None, ALU.mult))
            pool(lambda e: e.tensor_tensor(t8(1), ltb, t8(0), ALU.subtract))
            pool(lambda e: e.tensor_scalar(t8(0), ltb, 0.0, None, ALU.max))
            pool(lambda e: e.tensor_scalar(t8(1), t8(0), -2.0, None, ALU.mult))
            pool(lambda e: e.tensor_tensor(t8(1), ltb, t8(1), ALU.add))
            pool(lambda e: e.memset(t8(2), 2.718281828459045))
            pool(lambda e: e.tensor_tensor(t8(3), t8(2), t8(1), ALU.pow))
            pool(lambda e: e.tensor_scalar(t8(3), t8(3), 1.0, None, ALU.add))
            need("act", ("cp", chain[0] - 1))
            put("act", lambda e: e.activation(t8(4), t8(3), ACT.Ln), "ln", 0)
            need("pool", ("ln", 0))
            pool(lambda e: e.tensor_scalar(t8(5), t8(4), -1.0, None, ALU.mult))
            pool(lambda e: e.tensor_tensor(t8(5), t8(2), t8(5), ALU.pow))
            pool(lambda e: e.tensor_tensor(t8(5), t8(5), t8(3), ALU.mult))
            pool(lambda e: e.tensor_scalar(t8(5), t8(5), 1.0, None, ALU.subtract))
            pool(lambda e: e.tensor_tensor(t8(4), t8(4), t8(5), ALU.add))
            pool(lambda e: e.tensor_tensor(t8(4), t8(4), t8(0), ALU.add))
            pool(lambda e: e.tensor_scalar(t8(4), t8(4), 0.1, None, ALU.add))
            need("dve", ("cp", chain[0] - 1), ("w", 0))
            dve(lambda e: e.reciprocal(t8(8), t8(4)))
            dve(lambda e: e.tensor_scalar(U[:, :], U[:, :], tmp8[:, 8:9], None, ALU.mult))
            for c in range(2):
                dve(lambda e, c=c: e.tensor_scalar(wc[:, c, :], wc[:, c, :], wcs[:, c:c + 1], None, ALU.mult))
            dve(lambda e: e.tensor_scalar(wc[0:64, 2, :], wc[0:64, 2, :], wcs[0:64, 2:3], None, ALU.mult))
            g0, g1 = HN[:, 0, 0:R], HN[:, 1, 0:R]
            dve(lambda e: e.tensor_scalar(g0, rbB, 1.0 / TWO_PI, MAGIC, ALU.mult, ALU.add))
            dve(lambda e: e.tensor_scalar(g0, g0, MAGIC, None, ALU.subtract))
            dve(lambda e: e.scalar_tensor_tensor(g1, g0, -PI_HI, rbB, ALU.mult, ALU.add))
            dve(lambda e: e.scalar_tensor_tensor(biasC[:, 1, :], g0, -PI_LO, g1, ALU.mult, ALU.add))
            dve(lambda e: e.tensor_scalar(biasC[:, 0, :], biasC[:, 1, :], TWO_PI / 4, None, ALU.add))
            for eng in ("pe", "act", "dve", "pool"):
                need(eng, ("cd", dch[0] - 1))

        def slot_setup():
            need("pool", ("wf", 0))
            pool(lambda e: e.tensor_scalar(t8(6), taub, -1.0, None, ALU.mult))
            pool(lambda e: e.tensor_tensor(t8(6), taub, t8(6), ALU.subtract))
            pool(lambda e: e.tensor_scalar(t8(7), taub, 0.0, None, ALU.max))
            pool(lambda e: e.tensor_scalar(t8(7), t8(7), 2.0, None, ALU.mult))
            pool(lambda e: e.tensor_tensor(t8(7), t8(7), taub, ALU.subtract))
            pool(lambda e: e.tensor_scalar(t8(7), t8(7), 0.1, None, ALU.add))

            pool(lambda e: e.tensor_tensor(S0[:, :, :], S0[:, :, :],
                                           sscale.unsqueeze(1).broadcast_to([128, 2, S]), ALU.mult))
            pool(lambda e: e.tensor_copy(bcB, fbvc.unsqueeze(2).broadcast_to([128, 2, 128])))
            pool_done = ("cp", chain[0] - 1)
            need("dve", pool_done, ("wf", 0))
            dve(lambda e: e.reciprocal(t8(9), t8(7)))
            dve(lambda e: e.tensor_scalar(w2[:, :], w2[:, :], t8(9), None, ALU.mult))
            dve(lambda e: e.tensor_scalar(b2[:, :], b2raw, t8(9), None, ALU.mult))
            dve(lambda e: e.tensor_reduce(mslot, S0[:, :, :], AX.X, ALU.add))
            dve(lambda e: e.tensor_scalar(mslot, mslot, 1.0 / S, None, ALU.mult))
            dve(lambda e: e.tensor_tensor(bhh[:, 0:4], bhh[:, 0:4], bihn[:, 0:4], ALU.add))
            yield
            need("pe", pool_done, ("cd", dch[0] - 1), ("wf", 0))
            for c in range(2):
                cs = slice(c * 128, c * 128 + 128)
                setup_mm([(fwv[:, k, cs], fwoT[:, k, :]) for k in range(2)],
                         lambda e, p, c=c: e.tensor_copy(Wvo[:, c, :], p[:, 0:256]))
                yield
            setup_mm([(bcB[:, k, :], fwoT[:, k, :]) for k in range(2)] + [(ones[0:1, :], fbor)],
                     lambda e, p: e.tensor_copy(bSV[:, :], p[:, 0:256]))
            yield
            setup_mm([(w1b[:, k, :], mslot[:, k:k + 1]) for k in range(2)],
                     lambda e, p: e.tensor_tensor(b1[:, :], b1[:, :], p[:, 0:1], ALU.add))
            yield
            for j in range(6):
                setup_mm([(whh[:, k, j * 128:j * 128 + 128], S0[:, k, :]) for k in range(2)],
                         lambda e, p, j=j: e.tensor_scalar(GH[:, j, :], p[:, 0:S], bhh[:, j:j + 1], None, ALU.add))
                if j % 2:
                    yield
            dve(lambda e: e.tensor_scalar(HN[:, :, :], GH[:, 4:6, :], 0.5, None, ALU.mult))
            for eng in ("pe", "act", "pool"):
                need(eng, ("cd", dch[0] - 1))
            setup_done.extend([("cd", dch[0] - 1), ("cp", chain[0] - 1)])
            yield

        def transposed(srcs, p_src, evac_eng, evac, name, n):
            i, p = T.take()
            need("pe", *p_src)
            for j, s in enumerate(srcs):
                m = s.shape[-1]
                fn = lambda e, j=j, s=s, m=m, p=p: e.transpose(p[0:m, j * 128:j * 128 + 128], s, ident[:, :])
                put("pe", fn, *((name + "_t", n) if j == len(srcs) - 1 else ()))
            need(evac_eng, (name + "_t", n))
            put(evac_eng, lambda e, p=p: evac(e, p), name, n)
            T.freed[i] = (name, n)
            return i, p

        def norm2(b):
            norm(X[:, b % NX, :, :], ("x1", b), b, mv2, rs2, xm[:, b % 4, :, :], "lm",
                 [("xmT", 2 * (b - 4) + 1), ("gi_mm", b - 4)])

        def front(k):
            bs = (2 * k, 2 * k + 1)
            for b in bs:
                d = b % 2
                for c in range(2):
                    need("act", ("vs_mm", 4 * (b - 2) + 3))
                    i, p = transposed([xn[:, d, t, c * 128:c * 128 + 128] for t in range(4)], [("ln_n", b)],
                                      "act", lambda e, p, c=c, d=d: e.activation(xh[:, d, c, :], p[:, :], ACT.Copy),
                                      "xnT", 2 * b + c)
                    need("dve", ("xnT", 2 * b + c), ("vs_mm", 4 * (b - 2) + 3))
                    put("dve", lambda e, c=c, d=d, p=p: e.tensor_tensor(
                        xl[:, d, c, :], p[:, :], xh[:, d, c, :].bitcast(FP), ALU.subtract), "xl", 2 * b + c)
                    T.freed[i] = ("xl", 2 * b + c)
                    yield
            for b in bs:
                d = b % 2
                for t in range(4):
                    i, p = G.take()
                    need("pe", ("xnT", 2 * b + 1), ("xl", 2 * b + 1), projection)
                    parts = [(x, w, c) for c in range(2) for x, w in ((xh, W1h), (xh, W1l), (xl, W1h))]
                    for j, (x, w, c) in enumerate(parts):
                        put("pe", lambda e, x=x, w=w, c=c, j=j, t=t, p=p, d=d: e.matmul(
                            p[:, 0:FEATS], x[:, d, c, t * 128:t * 128 + 128], w[:, c, :],
                            start=j == 0, stop=j == 5), *(("vs_mm", 4 * b + t) if j == 5 else ()))
                    need("dve", ("vs_mm", 4 * b + t), projection, ("av", 4 * (b - 4) + 3), ("trig", b // 2 - 2), ("q2", b // 2 - 2))
                    put("dve", lambda e, t=t, p=p, b=b: e.tensor_tensor(VS[:, b % 4, t, :], p[:, 0:FEATS],
                                                                       biasM[:, :], ALU.add), "vs", 4 * b + t)
                    G.freed[i] = ("vs", 4 * b + t)
                    yield
            if k == 0:
                attn_setup()
            v0 = (2 * k) % 4
            VP = VS[:, v0:v0 + 2, :, :]
            need("act", ("vs", 4 * bs[1] + 3), ("tp", bs[1] - 2))
            put("act", lambda e: e.activation(qq[:, :, :, 0:1], VP[:, :, :, 320:321], ACT.Tanh), "q1", k)
            for b in bs:
                d = b % 2
                need("pool", ("vs", 4 * b + 3), ("sin", k - 1))
                put("pool", lambda e, b=b, d=d: e.tensor_tensor(tg[:, d, :, :], VS[:, b % 4, :, 256:320],
                                                               VS[:, b % 4, :, 256:320], ALU.mult), "sq", b)
                need("dve", ("sq", b))
                put("dve", lambda e, d=d: e.tensor_reduce(n2[:, d, 0, :], tg[:, d, :, :], AX.X, ALU.add), "n2", b)
            need("pool", ("n2", bs[1]))
            put("pool", lambda e: e.tensor_scalar(n2[:, :, 1, :], n2[:, :, 0, :], 1e-24, None, ALU.max), "n2m", k)
            need("pool", ("n2m", k))
            put("pool", lambda e: e.tensor_tensor(n2[:, :, 0, :], n2[:, :, 1, :],
                                                  half[:, :].rearrange("p (a b) -> p a b", a=2), ALU.pow), "rn", k)
            need("pool", ("q1", k))
            put("pool", lambda e: e.tensor_tensor(qq[:, :, :, 1:2], qq[:, :, :, 0:1], qq[:, :, :, 0:1], ALU.mult),
                "q2", k)
            need("pool", ("q2", k))
            put("pool", lambda e: e.tensor_tensor(qq[:, :, :, 2:4], qq[:, :, :, 0:2],
                                                  qq[:, :, :, 1:2].broadcast_to([128, 2, 4, 2]), ALU.mult), "q4", k)
            yield
            for b in bs:
                d = b % 2
                need("dve", ("rn", k))
                put("dve", lambda e, b=b, d=d: e.tensor_tensor(
                    tg2[:, d, :, 0:R], VS[:, b % 4, :, 321:353],
                    n2[:, d, 0, :].unsqueeze(2).broadcast_to([128, 4, R]), ALU.mult), "p1", b)
                need("dve", ("p1", b))
                put("dve", lambda e, d=d: e.tensor_tensor(
                    tg[:, d, :, :].rearrange("p t (a r) -> p t a r", a=2),
                    tg2[:, d, :, 0:R].unsqueeze(2).broadcast_to([128, 4, 2, R]),
                    biasC[:, :, :].unsqueeze(1).broadcast_to([128, 4, 2, R]), ALU.add), "p2", b)
            f = lambda z: z[:, :, :, :].rearrange("p d t r -> p (d t r)")
            steps = [
                lambda e: e.tensor_scalar(f(tg2), f(tg), 1.0 / TWO_PI, MAGIC, ALU.mult, ALU.add),
                lambda e: e.tensor_scalar(f(tg2), f(tg2), MAGIC, None, ALU.subtract),
                lambda e: e.scalar_tensor_tensor(f(tg), f(tg2), -PI_HI, f(tg), ALU.mult, ALU.add),
                lambda e: e.scalar_tensor_tensor(f(tg), f(tg2), -PI_LO, f(tg), ALU.mult, ALU.add),
                lambda e: e.tensor_scalar(f(tg), f(tg), PI_CLAMP, -PI_CLAMP, ALU.min, ALU.max),
            ]
            need("dve", ("p2", bs[1]))
            for j, s in enumerate(steps):
                put("dve", s, *(("p3", 5 * k + j) if j < 4 else ("trig", k)))
                if j < 4:
                    need("dve", ("p3", 5 * k + j))
                if j == 1 or j == 3:
                    yield
            yield
            yield
            need("act", ("trig", k), ("tp", bs[1] - 2), ("tpT_t", 3 * (bs[1] - 2) + 2))
            put("act", lambda e: e.activation(tp[:, :, :, 0, :], tg[:, :, :, :], ACT.Sin), "sin", k)
            for b in bs:
                d = b % 2
                need("pool", ("sin", k), ("q4", k), ("tpT_t", 3 * (b - 2) + 2))
                put("pool", lambda e, d=d: e.tensor_tensor(
                    tp[:, d, :, 1:5, :], tp[:, d, :, 0:1, :].broadcast_to([128, 4, 4, 64]),
                    qq[:, d, :, :].unsqueeze(3).broadcast_to([128, 4, 4, 64]), ALU.mult), "tp", b)
                yield

        def combine(k):
            bs = (2 * k, 2 * k + 1)
            for b in bs:
                d = b % 2
                tv = tp[:, d, :, :, :].rearrange("p t m r -> p t (m r)")
                for j in range(3):
                    w = 128 if j < 2 else 64
                    need("act", ("phi", k - 1), ("Ql", k - 1), ("qk", k - 1), ("h_mm", b - 4))
                    transposed([tv[:, t, j * 128:j * 128 + w] for t in range(4)], [("tp", b)], "act",
                               lambda e, p, j=j, w=w, d=d: e.activation(tpT(d, j)[0:w, :], p[0:w, :], ACT.Copy),
                               "tpT", 3 * b + j)
                    yield
            i, p = G.take()
            for j in range(3):
                w = 128 if j < 2 else 64
                for b in bs:
                    d = b % 2
                    need("pe", ("tpT", 3 * b + j))
                    put("pe", lambda e, j=j, w=w, p=p, d=d: e.matmul(
                        p[64 * d:64 * d + C, :], wc[0:w, j, :], tpT(d, j)[0:w, :], start=j == 0, stop=j == 2),
                        *(("phi", k) if j == 2 and b == bs[1] else ()))
            QF, KF, QR, KR = xmT[:, 0, 0, :], xmT[:, 0, 1, :], xmT[:, 1, 0, :], xmT[:, 1, 1, :]
            need("dve", ("phi", k))
            put("dve", lambda e, p=p: e.tensor_tensor(QF, p[:, :], U[:, :], ALU.mult), "QF", k)
            put("dve", lambda e, p=p: e.tensor_tensor(KF, p[:, :], Wk[:, :], ALU.mult), "KF", k)
            G.freed[i] = ("KF", k)
            for full, hi, name in ((QF, QR, "Q"), (KF, KR, "K")):
                need("act", (name + "F", k))
                put("act", lambda e, full=full, hi=hi: e.activation(hi.bitcast(FR), full, ACT.Copy), name + "h", k)
            for full, hi, lo, name, eng in ((QF, QR, Ql, "Q", "pool"), (KF, KR, Kl, "K", "pool")):
                need(eng, (name + "h", k), ("lg_mm", 8 * (k - 1) + 7))
                put(eng, lambda e, full=full, hi=hi, lo=lo: e.tensor_tensor(lo[:, :], full, hi, ALU.subtract),
                    name + "l", k)
            need("sp", ("Qh", k), ("Kh", k), ("lg_mm", 8 * (k - 1) + 7))
            moves = [(QS, own, QR), (QS, oth, QR), (KS, own, KR), (KS, oth, Kl[:, :].bitcast(FP))]
            for m, (dst, to, src) in enumerate(moves):
                if m == 3:
                    need("sp", ("Kl", k))
                for d in range(2):
                    put("sp", lambda e, d=d, dst=dst, to=to, src=src: e.dma_start(
                        dst[to(d), d, :].bitcast(FP), src[own(d), :]), "qk", k, by=16)
            yield

        def attn(k):
            banks_of = {}
            rows = [(b, i) for b in (2 * k, 2 * k + 1) for i in range(4)]

            def logits(b, i):
                r = 4 * b + i
                w = (i + 1) * 128
                bi, p = L.take()
                need("pe", ("qk", k), ("Ql", k))
                d, wide = b % 2, max(w, 256)
                put("pe", lambda e: e.matmul(p[:, 0:wide], QS[:, d, i * 128:w], KS[:, d, 0:wide],
                                             start=True, stop=False, skip_group_check=True))
                put("pe", lambda e: e.matmul(p[:, 0:wide], Ql[own(d), i * 128:w], KS[own(d), d, 0:wide],
                                             start=False, stop=False, skip_group_check=True))
                put("pe", lambda e: e.matmul(p[:, i * 128:w], identb[:, :], maskb[:, :], start=False, stop=True,
                                             skip_group_check=True), "lg_mm", r)
                need("dve", ("lg_mm", r), ("E", r - 8))
                put("dve", lambda e: e.tensor_reduce(nmax[:, r % 8:r % 8 + 1], p[:, 0:w], AX.X, ALU.max,
                                                     negate=True), "nmax", r)
                banks_of[r] = (bi, p)

            def expo(b, i):
                r = 4 * b + i
                w = (i + 1) * 128
                bi, p = banks_of[r]
                need("act", ("nmax", r), ("ET_t", r - 3), ("av", r - 8))
                put("act", lambda e: e.activation(E[:, r % 3, 0:w], p[:, 0:w], ACT.Exp,
                                                  bias=nmax[:, r % 8:r % 8 + 1],
                                                  accum_out=rsum[:, r % 8:r % 8 + 1]), "E", r)
                L.freed[bi] = ("E", r)

            def probs(b, i):
                r = 4 * b + i
                w = (i + 1) * 128
                need("act", ("av_mm", r - 2))
                transposed([E[:, r % 3, j * 128:j * 128 + 128] for j in range(i + 1)], [("E", r)], "act",
                           lambda e, p: e.activation(ET[:, r % 2, 0:w], p[:, 0:w], ACT.Copy), "ET", r)

            def values(b, i):
                r = 4 * b + i
                bi, p = G.take()
                need("pe", ("ET", r), ("vs", 4 * b + 3))
                for j in range(i + 1):
                    put("pe", lambda e, j=j: e.matmul(p[:, 0:D], ET[:, r % 2, j * 128:j * 128 + 128],
                                                      VS[:, b % 4, j, 0:256], start=j == 0, stop=j == i),
                        *(("av_mm", r) if j == i else ()))
                need("dve", ("E", r))
                put("dve", lambda e: e.reciprocal(rinv[:, r % 8:r % 8 + 1], rsum[:, r % 8:r % 8 + 1]), "rinv", r)
                need("dve", ("av_mm", r), ("rinv", r), ("ln_n", b))
                put("dve", lambda e: e.scalar_tensor_tensor(
                    X[:, b % NX, i, :], p[:, 0:D], rinv[:, r % 8:r % 8 + 1], X[:, b % NX, i, :],
                    ALU.mult, ALU.add), "av", r)
                G.freed[bi] = ("av", r)
                if i == 3:
                    q.at[("x1", b)] = q.at[("av", r)]

            for n in range(len(rows) + 4):
                if 1 <= n <= len(rows):
                    expo(*rows[n - 1])
                if n < len(rows):
                    logits(*rows[n])
                yield
                if 2 <= n <= len(rows) + 1:
                    probs(*rows[n - 2])
                yield
                if 3 <= n <= len(rows) + 2:
                    values(*rows[n - 3])
                yield
                if n >= 4:
                    b, i = rows[n - 4]
                    stat(X[:, b % NX, :, :], i, ("av", 4 * b + i), b, stats2, "lm")
                    if i:
                        aggr(i - 1, b, stats2, mv2, "lm")
                    if i == 3:
                        aggr(i, b, stats2, mv2, "lm")
                        norm2(b)
                yield

        def back(k):
            bs = (2 * k, 2 * k + 1)
            for b in bs:
                d = b % 2
                for c in range(2):
                    need("act", ("h_mm", b - 2), ("Ql", min(k + 1, B // 2 - 1)), ("qk", min(k + 1, B // 2 - 1)))
                    transposed([xm[:, b % 4, t, c * 128:c * 128 + 128] for t in range(4)], [("lm_n", b)], "act",
                               lambda e, p, c=c, d=d: e.activation(xmT[:, d, c, :], p[:, :], ACT.Copy),
                               "xmT", 2 * b + c)
                    yield
            held = []
            for b in bs:
                d = b % 2
                i, p = G.take()
                held.append((i, p))
                need("pe", ("xmT", 2 * b + 1))
                for c in range(2):
                    put("pe", lambda e, c=c, p=p, d=d: e.matmul(p[:, :], w1a[:, c, :], xmT[:, d, c, :],
                                                              start=c == 0, stop=c == 1),
                        *(("h_mm", b) if c else ()))
            for b, (i, p) in zip(bs, held):
                d = b % 2
                need("act", ("h_mm", b), ("rt_mm", b - 2))
                put("act", lambda e, p=p, d=d: e.activation(hT[:, d, :], p[:, :], ACT.Gelu, bias=b1[:, 0:1]), "h", b)
                G.freed[i] = ("h", b)
            yield
            for b in bs:
                d = b % 2
                i, p = G.take()
                need("pe", ("h", b))
                for t in range(4):
                    put("pe", lambda e, t=t, p=p, d=d: e.matmul(p[:, t * S:t * S + S], hT[:, d, t * 128:t * 128 + 128],
                                                              w2[:, :], start=True, stop=True, skip_group_check=True),
                        *(("rt_mm", b) if t == 3 else ()))
                need("dve", ("rt_mm", b), ("al", b - 2))
                put("dve", lambda e, p=p, d=d: e.tensor_tensor(
                    lg[:, d, 0, :, :], p[:, 0:4 * S].rearrange("p (t s) -> p t s", t=4),
                    b2[:, :].unsqueeze(1).broadcast_to([128, 4, S]), ALU.add), "lg", b)
                G.freed[i] = ("lg", b)
                yield
                need("dve", ("lg", b))
                for t in range(4):
                    put("dve", lambda e, t=t, d=d: e.max(m8[:, d, t, :], lg[:, d, 0, t, :]), "m8", 4 * b + t)
                for t in range(4):
                    need("dve", ("m8", 4 * b + t))
                    put("dve", lambda e, t=t, d=d: e.match_replace(lg[:, d, 1, t, :], m8[:, d, t, :],
                                                                  lg[:, d, 0, t, :], -3e38), "mr", 4 * b + t)
                need("pool", ("mr", 4 * b + 3))
                for z in range(2):
                    put("pool", lambda e, d=d, z=z: e.tensor_tensor(
                        lg[:, d, z, :, :], lg[:, d, z, :, :],
                        m8[:, d, :, 0:1].broadcast_to([128, 4, S]), ALU.subtract), *(("dm", b) if z else ()))
                yield
            for b in bs:
                d = b % 2
                need("act", ("dm", b))
                put("act", lambda e, d=d: e.activation(lg[:, d, :, :, :], lg[:, d, :, :, :], ACT.Exp), "ex", b)
                need("pool", ("ex", b))
                put("pool", lambda e, d=d: e.tensor_tensor(lg[:, d, 0, :, :], lg[:, d, 0, :, :], lg[:, d, 1, :, :],
                                                          ALU.subtract), "am0", b)
                yield
            for _ in range(PAUSE):
                yield
            for b in bs:
                d = b % 2
                need("dve", ("am0", b))
                put("dve", lambda e, d=d: e.tensor_reduce(asum[:, d, 0, :], lg[:, d, 0, :, :], AX.X, ALU.add),
                    "as0", b)
                need("dve", ("as0", b))
                put("dve", lambda e, d=d: e.reciprocal(asum[:, d, 1, :], asum[:, d, 0, :]), "as1", b)
                need("pool", ("as1", b), ("aT_t", k - 2), ("gi_mm", b - 4))
                put("pool", lambda e, d=d: e.tensor_tensor(
                    AL[:, k % 2, :, d, :], lg[:, d, 0, :, :],
                    asum[:, d, 1, :].unsqueeze(2).broadcast_to([128, 4, S]), ALU.mult), "am", b)
                need("pool", ("am", b), ("gi_mm", b - 2))
                put("pool", lambda e, d=d: e.tensor_tensor(lg[:, d, 1, 0:2, :], AL[:, k % 2, 0:2, d, :],
                                                          AL[:, k % 2, 2:4, d, :], ALU.add), "al0", b)
                need("pool", ("al0", b))
                put("pool", lambda e, d=d: e.tensor_tensor(alt[:, d, :], lg[:, d, 1, 0, :], lg[:, d, 1, 1, :],
                                                          ALU.add), "al", b)
                yield
            for b in bs:
                d = b % 2
                i, p = G.take()
                need("pe", ("am", b), ("al", b), ("lm_n", b))
                for c in range(2):
                    for t in range(4):
                        put("pe", lambda e, c=c, t=t, p=p, d=d, b=b: e.matmul(
                            p[:, c * S:c * S + S], xm[:, b % 4, t, c * 128:c * 128 + 128], AL[:, k % 2, t, d, :],
                            start=t == 0, stop=t == 3))
                put("pe", lambda e, p=p, d=d: e.matmul(p[:, 2 * S:3 * S], ones[:, :], alt[:, d, :],
                                                     start=True, stop=True), "gi_mm", b)
                need("dve", ("gi_mm", b), ("gi", b - 1))
                put("dve", lambda e, p=p: e.tensor_scalar(rw[:, :], p[:, 2 * S:3 * S], 1e-8, None, ALU.add), "rw0", b)
                need("dve", ("rw0", b))
                put("dve", lambda e: e.reciprocal(rw[:, :], rw[:, :]), "rw", b)
                need("dve", ("rw", b), ("gx_mm", k - 2))
                put("dve", lambda e, p=p, d=d: e.tensor_tensor(
                    GI[:, k % 2, :, d, :], p[:, 0:2 * S].rearrange("p (c s) -> p c s", c=2),
                    rw[:, :].unsqueeze(1).broadcast_to([128, 2, S]), ALU.mult), "gi", b)
                G.freed[i] = ("gi", b)
                yield

        def slots(k):
            i1, p1 = G.take()
            need("pe", ("gi", 2 * k + 1))
            gx = lambda j, c: (wih[:, c, j * 128:j * 128 + 128], GI[:, k % 2, c, :, :].rearrange("p b s -> p (b s)"))
            for j in range(4):
                for c in range(2):
                    put("pe", lambda e, j=j, c=c: e.matmul(p1[:, j * 128:j * 128 + 128], *gx(j, c),
                                                           start=c == 0, stop=c == 1),
                        *(("rz_mm", k) if j == 3 and c else ()))
            need("dve", ("rz_mm", k), ("as", k - 1))
            put("dve", lambda e: e.tensor_tensor(
                grz[:, :, :, :], p1[:, :].rearrange("p (j b s) -> p j b s", j=4, b=2),
                GH[:, 0:4, :].unsqueeze(2).broadcast_to([128, 4, 2, S]), ALU.add), "grz", k)
            G.freed[i1] = ("grz", k)
            yield
            need("act", ("grz", k))
            fl = lambda z: z.rearrange("p c b s -> p (c b s)")
            put("act", lambda e: e.activation(fl(grz[:, :, :, :]), fl(grz[:, :, :, :]), ACT.Tanh, scale=0.5), "srz", k)
            yield
            i2, p2 = G.take()
            for j in range(2):
                for c in range(2):
                    put("pe", lambda e, j=j, c=c: e.matmul(p2[:, j * 128:j * 128 + 128], *gx(4 + j, c),
                                                           start=c == 0, stop=c == 1),
                        *(("gx_mm", k) if j and c else ()))
            need("dve", ("srz", k), ("SVl", k - 1))
            put("dve", lambda e: e.scalar_tensor_tensor(
                gt[:, 0, :, :], grz[:, 0, :, :], 1.0,
                HN[:, 0, :].unsqueeze(1).broadcast_to([128, 2, S]), ALU.add, ALU.mult))
            put("dve", lambda e: e.scalar_tensor_tensor(
                gt[:, 1, :, :], grz[:, 1, :, :], 1.0,
                HN[:, 1, :].unsqueeze(1).broadcast_to([128, 2, S]), ALU.add, ALU.mult), "rhn", k)
            need("dve", ("rhn", k), ("gx_mm", k))
            put("dve", lambda e: e.tensor_tensor(fl(gn[:, :, :, :]), p2[:, 0:256], fl(gt[:, :, :, :]), ALU.add),
                "gn", k)
            G.freed[i2] = ("gn", k)
            need("act", ("gn", k))
            for c in range(2):
                put("act", lambda e, c=c: e.activation(gn[:, c, :, :], gn[:, c, :, :], ACT.Tanh,
                                                       bias=bihn[:, 4 + c:5 + c]), *(("nn", k) if c else ()))
            yield
            need("pool", ("nn", k))
            put("pool", lambda e: e.tensor_tensor(
                gt[:, :, :, :], S0[:, :, :].unsqueeze(2).broadcast_to([128, 2, 2, S]), gn[:, :, :, :],
                ALU.subtract), "hd", k)
            yield
            need("dve", ("hd", k))
            put("dve", lambda e: e.scalar_tensor_tensor(fl(gt[:, :, :, :]), fl(grz[:, 2:4, :, :]), 1.0,
                                                        fl(gt[:, :, :, :]), ALU.add, ALU.mult), "hz", k)
            need("dve", ("hz", k), ("sv_mm", k - 1))
            put("dve", lambda e: e.scalar_tensor_tensor(fl(SN[:, :, :, :]), fl(gt[:, :, :, :]), 0.5,
                                                        fl(gn[:, :, :, :]), ALU.mult, ALU.add), "sn", k)
            aTR = grz[:, :, :, :].rearrange("p j b s -> p (j b s)")
            need("act", ("hz", k))
            ti, tpb = transposed([AL[:, k % 2, t, :, :].rearrange("p b s -> p (b s)") for t in range(4)],
                                 [("am", 2 * k + 1)], "act",
                                 lambda e, p: e.activation(aTR.bitcast(FR), p[:, :], ACT.Copy), "aT", k)
            need("dve", ("aT", k), ("of_mm", 4 * (k - 1) + 3))
            put("dve", lambda e: e.tensor_tensor(aTl[:, :], tpb[:, :], aTR, ALU.subtract), "aTl", k)
            T.freed[ti] = ("aTl", k)
            need("sp", ("aT", k), ("of_mm", 4 * (k - 1) + 3))
            for to, src in ((own, aTR), (oth, aTl[:, :].bitcast(FP))):
                if to is oth:
                    need("sp", ("aTl", k))
                for d in range(2):
                    put("sp", lambda e, d=d, to=to, src=src: e.dma_start(AS[to(d), d, :].bitcast(FP), src[own(d), :]),
                        "as", k, by=16)
            yield
            i3, p3 = G.take()
            need("pe", ("sn", k))
            for c in range(2):
                put("pe", lambda e, c=c: e.matmul(p3[:, 0:D], SN[:, c, :, :].rearrange("p b s -> p (b s)"),
                                                  Wvo[:, c, :], start=c == 0, stop=c == 1),
                    *(("sv_mm", k) if c else ()))
            SVF, SVR = fl(gt[:, :, :, :]), fl(gn[:, :, :, :])
            need("dve", ("sv_mm", k), ("sn", k))
            put("dve", lambda e: e.tensor_tensor(SVF, p3[:, 0:D], bSV[:, :], ALU.add), "sv", k)
            G.freed[i3] = ("sv", k)
            need("act", ("sv", k))
            put("act", lambda e: e.activation(SVR.bitcast(FR), SVF, ACT.Copy), "SVh", k)
            need("sp", ("SVh", k))
            for to in (own, oth):
                for d in range(2):
                    put("sp", lambda e, d=d, to=to: e.dma_start(SVS[to(d), d, :].bitcast(FP), SVR[own(d), :]),
                        "as", k, by=16)
            need("pool", ("SVh", k), ("of_mm", 4 * (k - 1) + 3))
            put("pool", lambda e: e.tensor_tensor(SVl[:, :], SVF, SVR, ALU.subtract), "SVl", k)
            yield
            yield
            for b in (2 * k, 2 * k + 1):
                d = b % 2
                for t in (0, 2):
                    bi, p = G.take()
                    need("pe", ("as", k), ("SVl", k))
                    for u in range(2):
                        put("pe", lambda e, t=t + u, u=u, p=p, d=d: e.matmul(
                            p[:, u * D:u * D + D], AS[:, d, t * 128:t * 128 + 128], SVS[:, d, :],
                            start=True, stop=False))
                        put("pe", lambda e, t=t + u, u=u, p=p, d=d: e.matmul(
                            p[:, u * D:u * D + D], AS[own(d), d, t * 128:t * 128 + 128], SVl[own(d), :],
                            start=False, stop=True), *(("of_mm", 2 * b + t // 2) if u else ()))
                    need("dve", ("of_mm", 2 * b + t // 2), ("lm_n", b))
                    xv = X[:, b % NX, t:t + 2, :]
                    put("dve", lambda e, xv=xv, p=p: e.tensor_tensor(
                        xv, p[:, :].rearrange("p (t d) -> p t d", t=2), xv, ALU.add), "fin", 2 * b + t // 2)
                    G.freed[bi] = ("fin", 2 * b + t // 2)
                    if t == 0:
                        yield
                need("sp", ("fin", 2 * b + 1))
                put("sp", lambda e, b=b: e.dma_start(out[b].rearrange("(t p) d -> p t d", p=128), X[:, b % NX, :, :]),
                    "st", b, sem=f"st{b % NX}", by=16)
                yield

        NP = B // 2
        for it in range(NP + 3):
            work = [(kind, stage(it - lag)) for kind, stage, lag in
                    (("F", front, 0), ("C", combine, 0), ("N", norm1, -1), ("A", attn, 1), ("B", back, 2), ("S", slots, 3))
                    if 0 <= it - lag < NP]
            if it == 0:
                work.append(("W", slot_setup()))
            turns = sorted((at, n) for n, (kind, _) in enumerate(work) for at in PLACES[kind])
            for _, n in turns:
                next(work[n][1])
            for kind, g in work:
                assert next(g, "end") == "end", kind
            for b in (2 * it + 4, 2 * it + 5):
                if b < B:
                    load_x(b)
        need("sp", *[("st", b) for b in range(B)])

        block = ctx.enter_context(nc.Block())

        @block.sync
        def _(e):
            for fn in q.lists["sp"]:
                fn(e)

        @block.gpsimd
        def _(e):
            for fn in q.lists["pool"]:
                fn(e)

        @block.scalar
        def _(e):
            for fn in q.lists["act"]:
                fn(e)

        @block.vector
        def _(e):
            for fn in q.lists["dve"]:
                fn(e)

        @block.tensor
        def _(e):
            for fn in q.lists["pe"]:
                fn(e)


PAUSE = 1
PLACES = dict(
    F=(0.000, 0.000, 0.000, 0.002, 0.002, 0.002, 0.002, 0.002, 0.002, 0.003, 0.022, 0.038, 0.049, 0.206,
       0.229, 0.251, 0.254, 0.260, 0.284),
    C=(0.480, 0.502, 0.630, 0.658, 0.660, 0.718, 0.777),
    N=(0.441, 0.510, 0.636, 0.680, 0.688, 0.749),
    A=(0.044, 0.044, 0.072, 0.077, 0.080, 0.138, 0.143, 0.146, 0.156, 0.169, 0.204, 0.223, 0.237, 0.289,
       0.303, 0.315, 0.338, 0.401, 0.464, 0.494, 0.496, 0.496, 0.497, 0.503, 0.506, 0.534, 0.534, 0.558,
       0.619, 0.629, 0.670, 0.676, 0.692, 0.699, 0.713, 0.753, 0.769, 0.772, 0.783, 0.788, 0.799, 0.801,
       0.813, 0.841, 0.849, 0.855, 0.855, 0.961),
    B=(0.014, 0.149, 0.204, 0.229, 0.243, 0.372, 0.427, 0.451, 0.466, 0.522, 0.524, 0.633, 0.660, 0.671,
       0.988, 0.989),
    S=(0.001, 0.113, 0.178, 0.232, 0.244, 0.345, 0.632, 0.979, 0.983, 1.000, 1.000),
    W=(0.006, 0.047, 0.085, 0.352, 0.403, 0.409, 0.411, 0.543, 0.846),
)


def kernel(**inputs):
    import concourse.bacc as bacc
    from concourse.bass_utils import run_bass_kernel_spmd

    g = {k: np.asarray(v) for k, v in inputs.items()}
    at, ff = "L0_attn_", "L0_ffn_"
    con = np.ascontiguousarray
    ramp = np.arange(N, dtype=np.float64) - (N - 1) / 2
    arrays = {
        "x": g[at + "x"],
        "b_charge": g[at + "b_charge"],
        "W_shell": g[at + "W_shell"],
        "W_scT": con(np.concatenate([g[at + "W_shell"], g[at + "W_charge"]]).T),
        "b_shell": g[at + "b_shell"],
        "omegaT": con(g[at + "omega"].T),
        "rff_bias": g[at + "rff_bias"],
        "W_combineT": con(g[at + "W_combine"].T),
        "W_v": g[at + "W_v"],
        "b_v": con(g[at + "b_v"].reshape(2, 128).T),
        "W_outT": con(g[at + "W_out"].T),
        "b_out": g[at + "b_out"],
        "log_temp": con(g[at + "log_temp"].reshape(1)),
        "decay": np.stack([np.exp(-0.03 * ramp), np.exp(0.03 * ramp)]).astype(np.float32),
        "slot_initT": con(g[ff + "slot_init"].T),
        "slot_scale": con(g[ff + "slot_scale"].reshape(-1)),
        "w1T": con(g[ff + "w1"].T),
        "b1": g[ff + "b1"],
        "w2T": con(g[ff + "w2"].T),
        "b2": g[ff + "b2"],
        "gru_wihT": con(g[ff + "gru_wih"].T),
        "gru_whhT": con(g[ff + "gru_whh"].T),
        "gru_bih": con(g[ff + "gru_bih"].reshape(6, 128).T),
        "gru_bhh": con(g[ff + "gru_bhh"].reshape(6, 128).T),
        "wv": g[ff + "wv"],
        "bv": con(g[ff + "bv"].reshape(2, 128).T),
        "woT": con(g[ff + "wo"].T),
        "bo": g[ff + "bo"],
        "tau": g[ff + "tau"],
    }
    nc = bacc.Bacc("TRN2", target_bir_lowering=False, num_devices=1)
    aps = {k: nc.dram_tensor("in_" + k, v.shape, mybir.dt.from_np(v.dtype), kind="ExternalInput").ap()
           for k, v in arrays.items()}
    out = nc.dram_tensor("out_x", (B, N, D), FP, kind="ExternalOutput").ap()
    build(nc, aps, out)
    r = run_bass_kernel_spmd(nc, [{"in_" + k: v for k, v in arrays.items()}], core_ids=[0])
    return r.results[0]["out_x"]
```
